# Optimizing a Trainium2 kernel written in Bass

```python
import numpy as np
import jax
import jax.numpy as jnp

def _softmax(x, axis=-1):
    return jax.nn.softmax(x, axis=axis)

def _gelu(x):
    return jax.nn.gelu(x, approximate=True)

def _silu(x):
    return jax.nn.silu(x)

def _sigmoid(x):
    return jax.nn.sigmoid(x)

def _layernorm(x, axis=-1, eps=1e-05):
    m = jnp.mean(x, axis=axis, keepdims=True)
    v = jnp.var(x, axis=axis, keepdims=True)
    return (x - m) / jnp.sqrt(v + eps)

def _scatter_add(tgt, idx, src, axis=0):
    return tgt.at[idx].add(src)

def _segment_sum(src, seg, n):
    return jax.ops.segment_sum(src, seg, n)
kernel_name = 'mk_adj_ffn_d1_adj_r2_1cf44f'

def setup_inputs(seed: int=0):
    np.random.seed(seed)
    _w = jnp.asarray

    def _rec_inputs():
        import jax
        import jax.numpy as jnp
        _gk = jax.random.key(seed)
        x = -0.0003929 + 0.9999 * jax.random.normal(jax.random.fold_in(_gk, 1), (32, 256, 128), jnp.float32)
        _w = (1.0 + jnp.arange(256, dtype=jnp.float32)) ** (-0.5)
        _w = _w / _w.mean()
        _pij = jnp.clip(0.0625 * _w[:, None] * _w[None, :], 0.0, 1.0)
        _a = jax.random.uniform(jax.random.fold_in(_gk, 2), (256, 256)) < _pij
        _a = jnp.logical_or(_a, jnp.swapaxes(_a, -1, -2))
        _a = jnp.logical_or(_a, jnp.eye(256, dtype=bool))
        _af = _a.astype(jnp.float32)
        _af = _af * jax.random.uniform(jax.random.fold_in(_gk, 3), (256, 256), jnp.float32, 0.05, 0.999963)
        adj = _af
        return (x, adj)
    x, adj = _rec_inputs()

    def _L0_gnn_setup():
        import jax, jax.numpy as jnp
        import numpy as np
        BT, N, D, HEADS, E = (512, 64, 128, 4, 256)
        LRELU_SLOPE = 0.2
        EPS = 1e-08
        key = jax.random.key(seed)
        ks = jax.random.split(key, 8)
        d = D
        return {'H': jax.random.normal(ks[0], (BT, N, d), jnp.float32), 'W_lin': jax.random.normal(ks[1], (d, d), jnp.float32) / np.sqrt(d).astype(np.float32), 'W_val': jax.random.normal(ks[2], (d, d), jnp.float32) / np.sqrt(d).astype(np.float32), 'a': jax.random.normal(ks[3], (HEADS, d // HEADS), jnp.float32), 'W_out': jax.random.normal(ks[4], (d, d), jnp.float32) / np.sqrt(d).astype(np.float32), 'A0': jax.random.uniform(ks[5], (N, N), jnp.float32), 'src': jax.random.randint(ks[6], (E,), 0, N, jnp.int32), 'dst': jax.random.randint(ks[7], (E,), 0, N, jnp.int32)}
    _L0_gnn_all = _L0_gnn_setup()
    _L0_gnn_in = {k: v for k, v in _L0_gnn_all.items() if k in ('W_lin', 'W_val', 'a', 'W_out', 'src', 'dst')}
    del _L0_gnn_all

    def _L0_ffn_setup():
        import math
        import jax, jax.numpy as jnp
        import numpy as np
        CAPACITY_FACTOR = 1.25
        TOP_K = 2
        LN_EPS = 1e-05

        def _layer_norm(x, gamma, beta):
            mu = jnp.mean(x, axis=-1, keepdims=True)
            var = jnp.var(x, axis=-1, keepdims=True)
            return (x - mu) * jax.lax.rsqrt(var + LN_EPS) * gamma + beta
        key = jax.random.key(seed)
        ks = jax.random.split(key, 4)
        B, S, D, F, E = (8, 2048, 128, 256, 8)
        x = jax.random.normal(ks[0], (B, S, D), dtype=jnp.float32)
        Wr = jax.random.normal(ks[1], (D, E), dtype=jnp.float32) / np.sqrt(D)
        br = jnp.zeros((E,), jnp.float32)
        W1 = jax.random.normal(ks[2], (E, D, F), dtype=jnp.float32) / np.sqrt(D)
        b1 = jnp.zeros((E, F), jnp.float32)
        W2 = jax.random.normal(ks[3], (E, F, D), dtype=jnp.float32) / np.sqrt(F)
        b2 = jnp.zeros((E, D), jnp.float32)
        gamma = jnp.ones((D,), jnp.float32)
        beta = jnp.zeros((D,), jnp.float32)
        return {'x': x, 'Wr': Wr, 'br': br, 'W1': W1, 'b1': b1, 'W2': W2, 'b2': b2, 'gamma': gamma, 'beta': beta}
    _L0_ffn_all = _L0_ffn_setup()
    _L0_ffn_in = {k: v for k, v in _L0_ffn_all.items() if k in ('Wr', 'br', 'W1', 'b1', 'W2', 'b2', 'gamma', 'beta')}
    del _L0_ffn_all
    return {'x': x, 'adj': adj, 'L0_gnn_W_lin': _L0_gnn_in['W_lin'], 'L0_gnn_W_val': _L0_gnn_in['W_val'], 'L0_gnn_a': _L0_gnn_in['a'], 'L0_gnn_W_out': _L0_gnn_in['W_out'], 'L0_gnn_src': _L0_gnn_in['src'], 'L0_gnn_dst': _L0_gnn_in['dst'], 'L0_ffn_Wr': _L0_ffn_in['Wr'], 'L0_ffn_br': _L0_ffn_in['br'], 'L0_ffn_W1': _L0_ffn_in['W1'], 'L0_ffn_b1': _L0_ffn_in['b1'], 'L0_ffn_W2': _L0_ffn_in['W2'], 'L0_ffn_b2': _L0_ffn_in['b2'], 'L0_ffn_gamma': _L0_ffn_in['gamma'], 'L0_ffn_beta': _L0_ffn_in['beta']}

def reference(x, adj, L0_gnn_W_lin, L0_gnn_W_val, L0_gnn_a, L0_gnn_W_out, L0_gnn_src, L0_gnn_dst, L0_ffn_Wr, L0_ffn_br, L0_ffn_W1, L0_ffn_b1, L0_ffn_W2, L0_ffn_b2, L0_ffn_gamma, L0_ffn_beta):
    import jax
    import jax.numpy as jnp

    def _L0_gnn_ref(H, W_lin, W_val, a, W_out, A0, src, dst):
        import jax, jax.numpy as jnp
        import numpy as np
        BT, N, D, HEADS, E = (512, 64, 128, 4, 256)
        LRELU_SLOPE = 0.2
        EPS = 1e-08
        bt, n, d = H.shape
        h, dh = a.shape
        Xq = (H @ W_lin.T).reshape(bt, n, h, dh)
        Xv = (H @ W_val.T).reshape(bt, n, h, dh)
        Qs = Xq[:, src]
        Kt = Xq[:, dst]
        e = jnp.einsum('behd,hd->beh', jax.nn.leaky_relu(Qs + Kt, LRELU_SLOPE), a)
        e = e + jnp.log(A0[src, dst] + EPS)[None, :, None]
        e_t = e.transpose(1, 0, 2)
        m = jax.ops.segment_max(e_t, src, num_segments=n)
        ex = jnp.exp(e_t - m[src])
        denom = jax.ops.segment_sum(ex, src, num_segments=n)
        attn = ex / denom[src]
        Vt = Xv[:, dst].transpose(1, 0, 2, 3)
        Y = jax.ops.segment_sum(attn[..., None] * Vt, src, num_segments=n)
        Y = Y.transpose(1, 0, 2, 3).reshape(bt, n, d)
        return Y @ W_out.T

    def _L0_ffn_ref(x, Wr, br, W1, b1, W2, b2, gamma, beta):
        import math
        import jax, jax.numpy as jnp
        import numpy as np
        CAPACITY_FACTOR = 1.25
        TOP_K = 2
        LN_EPS = 1e-05

        def _layer_norm(x, gamma, beta):
            mu = jnp.mean(x, axis=-1, keepdims=True)
            var = jnp.var(x, axis=-1, keepdims=True)
            return (x - mu) * jax.lax.rsqrt(var + LN_EPS) * gamma + beta
        B, S, D = x.shape
        E = Wr.shape[1]
        N = B * S
        K = TOP_K
        logits = jnp.mean(x, axis=1) @ Wr + br
        routing_weights = jax.nn.softmax(logits, axis=-1)
        capacity = float(math.ceil(N * CAPACITY_FACTOR / E))
        expected_loads = routing_weights.sum(axis=0) * (N / B)
        scale = jnp.where(expected_loads > capacity, capacity / expected_loads, 1.0)
        routing_weights = jax.nn.softmax(routing_weights * scale, axis=-1)
        rw_tok = jnp.broadcast_to(routing_weights[:, None, :], (B, S, E)).reshape(N, E)
        top_w, top_i = jax.lax.top_k(rw_tok, K)
        top_w = jax.nn.softmax(top_w, axis=-1)
        xf = x.reshape(N, D)
        h = jax.nn.gelu(jnp.einsum('nd,edf->enf', xf, W1) + b1[:, None, :], approximate=False)
        y = jnp.einsum('enf,efd->end', h, W2) + b2[:, None, :]
        w_dense = jnp.zeros((N, E), x.dtype).at[jnp.arange(N)[:, None], top_i].add(top_w)
        out = jnp.einsum('ne,end->nd', w_dense, y).reshape(B, S, D)
        out = _layer_norm(out + x, gamma, beta)
        return out
    x = x + _L0_gnn_ref(_layernorm(x, axis=-1), L0_gnn_W_lin, L0_gnn_W_val, L0_gnn_a, L0_gnn_W_out, adj, L0_gnn_src, L0_gnn_dst)
    x = x + _L0_ffn_ref(_layernorm(x, axis=-1), L0_ffn_Wr, L0_ffn_br, L0_ffn_W1, L0_ffn_b1, L0_ffn_W2, L0_ffn_b2, L0_ffn_gamma, L0_ffn_beta)
    return x

_drawn_inputs = setup_inputs


def setup_inputs(seed=0):
    import zlib

    import numpy as np

    out = dict(_drawn_inputs(seed))
    spreads = {'L0_ffn_br': (0.0, 0.1),
     'L0_ffn_b1': (0.0, 0.387),
     'L0_ffn_b2': (0.0, 0.287),
     'L0_ffn_gamma': (1.0, 0.2),
     'L0_ffn_beta': (0.0, 0.1)}
    factors = {}
    for name, (base, spread) in spreads.items():
        noise = np.random.default_rng([zlib.crc32(name.encode()), seed]).standard_normal(out[name].shape)
        drawn = base * np.exp(spread * noise) if base else spread * noise
        out[name] = jnp.asarray(drawn.astype(out[name].dtype))
    for name, factor in factors.items():
        out[name] = (out[name] * factor).astype(out[name].dtype)
    return out
```

```python
import concourse.bass as bass
from concourse import mybir
from contextlib import ExitStack


def gnn_moe_program(nc, x, adj, nets, a_col, router, experts, edges_row, edges_col, br, b2, gamma, beta, out):
    f32 = mybir.dt.float32
    f32r = mybir.dt.float32r
    i32 = mybir.dt.int32
    u32 = mybir.dt.uint32
    ALU = mybir.AluOpType
    ACT = mybir.ActivationFunctionType
    AX = mybir.AxisListType

    P = 128
    B, N, D = x.shape
    C = N // P
    E = edges_row.shape[1]
    K = E // P
    H = 4
    DH = D // H
    X = br.shape[0]
    F = (experts.shape[1] // X) // 2 // P * P
    FC = F // P
    EW = F + FC + FC * D
    TOP = 2
    ROWS = B * H
    CAPACITY = float(-(-B * N * 5 // 4 // X))
    SLOPE = 0.2
    LN_EPS = 1e-5
    LOG_EPS = 1e-8
    LOW = -1e30

    ctx = ExitStack()
    with ctx:
        def sb(name, shape, dt=f32):
            return ctx.enter_context(nc.sbuf_tensor(name, shape, dt))

        def sem(name):
            return ctx.enter_context(nc.semaphore(name))

        x_sb = sb("x_sb", [P, B * N // P * D])
        v_sb = sb("v_sb", [P, B * K * D])
        uT_sb = v_sb
        nets_sb = sb("nets_sb", [P, 3 * D])
        experts_sb = sb("experts_sb", [P, X * EW])
        gamma_sb = sb("gamma_sb", [P, D])
        beta_sb = sb("beta_sb", [P, D])
        router_sb = sb("router_sb", [P, X])
        br_sb = sb("br_sb", [B, X])
        b2_sb = sb("b2_sb", [X, D])
        adj_sb = sb("adj_sb", [P, C * N])
        a_sb = sb("a_sb", [P, 1])
        a_heads = sb("a_heads", [P, H])
        ident = sb("ident", [P, P])
        ones = sb("ones", [P, P])
        minus_half = sb("minus_half", [P, C])
        ln_eps = sb("ln_eps", [P, C])
        usum = sb("usum", [P, B])

        edges_row_i = sb("edges_row_i", [P, E], i32)
        edges_col_i = sb("edges_col_i", [P, 2 * K], i32)
        edges_col_f = sb("edges_col_f", [P, 2 * K])
        count_row = sb("count_row", [P, N])
        node_row = sb("node_row", [P, N])
        node_col = sb("node_col", [P, C])
        edge_col = sb("edge_col", [P, K])
        key_row = sb("key_row", [P, E])
        key_col = sb("key_col", [P, K])
        before = sb("before", [P, K * E])
        rank = sb("rank", [P, K])
        place = sb("place", [P, K * E])
        placed = sb("placed", [P, K * 2 * E])
        sorted_row = sb("sorted_row", [P, 2 * E])
        sorted_col = sb("sorted_col", [P, K * 2])
        source_of = sb("source_of", [P, C * E])
        target_of = sb("target_of", [P, C * E])
        gather = sb("gather", [P, C * 2 * E], f32r)
        spread = sb("spread", [P, K * N], f32r)
        target_hot = sb("target_hot", [P, K * N])
        adj_pick = sb("adj_pick", [P, K * N])
        log_adj = sb("log_adj", [P, K])
        same = sb("same", [P, E + 1])
        start_low = sb("start_low", [P, E])
        is_last = sb("is_last", [P, E])

        stats = sb("stats", [P, 2 * C * 6])
        mean_var = sb("mean_var", [P, 2 * C * 2])
        var_eps = sb("var_eps", [P, 2 * C])
        rstd = sb("rstd", [P, 2 * C])
        z = sb("z", [P, 2 * C * D])
        z_hi = sb("z_hi", [P, 2 * C * D], f32r)
        z_lo = sb("z_lo", [P, 2 * C * D], f32r)
        gathered = sb("gathered", [P, 2 * 2 * E])
        q_low = sb("q_low", [P, 2 * E])
        act_q = sb("act_q", [P, 2 * E])
        av = sb("av", [P, 2 * K * D])
        av_hi = sb("av_hi", [P, 2 * K * D], f32r)
        av_lo = sb("av_lo", [P, 2 * K * D], f32r)
        yT = sb("yT", [P, 2 * N])
        u = sb("u", [P, 2 * C * D])

        logits_e = sb("logits_e", [P, K * ROWS])
        logits = sb("logits", [ROWS, E])
        scan = sb("scan", [ROWS, E])
        at_last = sb("at_last", [ROWS, E])
        seg_max = sb("seg_max", [ROWS, E])
        shifted = sb("shifted", [ROWS, E])
        expo = sb("expo", [ROWS, E])
        seg_sum = sb("seg_sum", [ROWS, E])
        attn = sb("attn", [ROWS, E])
        attn_e = sb("attn_e", [P, K * ROWS])

        route = sb("route", [B, 24 * X])
        top_i = sb("top_i", [B, 8], u32)
        small = sb("small", [B, 16])
        spread_w = sb("spread_w", [B, B * 2 * TOP])
        dense_wT = sb("dense_wT", [X, B])
        weight_bc = sb("weight_bc", [P, B * 2 * TOP])
        offsets_i = sb("offsets_i", [P, B * 2 * TOP], i32)
        b2_mix = sb("b2_mix", [P, B])

        chosen = sb("chosen", [P, 2 * TOP * EW])
        hT = sb("hT", [P, 2 * TOP * FC * N])
        sT = sb("sT", [P, 2 * N])
        y = sb("y", [P, 2 * C * D])
        y_gamma = sb("y_gamma", [P, 2 * C * D])
        y_beta = sb("y_beta", [P, 2 * C * D])

        banks = [ctx.enter_context(nc.psum_tensor(f"bank{n}", [P, 512], f32)) for n in range(8)]

        XCH = 8
        s_edges, s_nets, s_adj, s_route_in, s_experts = (sem(n) for n in (
            "s_edges", "s_nets", "s_adj", "s_route_in", "s_experts"))
        s_x = [sem(f"s_x_in{n}") for n in range(XCH)]
        s_const, s_ident, s_prep, s_prep_pe, s_prep_act = (sem(n) for n in (
            "s_const", "s_ident", "s_prep", "s_prep_pe", "s_prep_act"))
        s_x_ready = sem("s_x_ready")
        s_stats, s_mv, s_ve, s_rstd, s_z, s_zhi, s_zlo, s_G, s_gt, s_q, s_vp, s_qlow, s_vs, s_lr, s_e = (
            sem(n) for n in ("s_stats", "s_mv", "s_ve", "s_rstd", "s_z", "s_zhi", "s_zlo", "s_G", "s_gt",
                             "s_q", "s_vp", "s_qlow", "s_vs", "s_lr", "s_e"))
        s_sm, s_sm_pe, s_sm_act = sem("s_sm"), sem("s_sm_pe"), sem("s_sm_act")
        s_av, s_avhi, s_avlo, s_y, s_ys, s_o, s_x1, s_u, s_t, s_ut = (
            sem(n) for n in ("s_av", "s_avhi", "s_avlo", "s_y", "s_ys", "s_o", "s_x1", "s_u", "s_t", "s_ut"))
        s_rt, s_rt_pe, s_rt_act = sem("s_rt"), sem("s_rt_pe"), sem("s_rt_act")
        s_sel, s_h, s_gelu, s_f, s_s, s_tr, s_yn, s_yg, s_yb, s_res, s_out = (
            sem(n) for n in ("s_sel", "s_h", "s_gelu", "s_f", "s_s", "s_tr", "s_yn", "s_yg", "s_yb",
                             "s_res", "s_out"))

        block = ctx.enter_context(nc.Block())

        def live(b):
            return not isinstance(b, int) or 0 <= b < B

        def from_second(b):
            return not isinstance(b, int) or b >= 2

        def turns(eng, lag, turn):
            head = lag + 2 + lag % 2
            for i in range(head):
                turn(i, i % 2)
            with eng.Fori(head // 2, B // 2) as j:
                turn(2 * j, 0)
                turn(2 * j + 1, 1)
            for i in range(B, B + lag):
                turn(i, i % 2)

        def cut(t, b, width, at=0, n=None):
            return t[:, bass.ds(b * width + at, width if n is None else n)]

        def halves(ap, n=2):
            return ap.rearrange("p (c d) -> p c d", c=n)

        W_LIN, W_VAL, W_OUT = (nets_sb[:, n * D:(n + 1) * D] for n in range(3))

        def layer_norm_scale(pool, done):
            def turn(b, s):
                mv = cut(mean_var, s, 2 * C).rearrange("p (c k) -> p c k", k=2)[:, :, 1]
                pool.wait_ge(s_mv, (done + b) * C + C)
                if done or from_second(b):
                    pool.wait_ge(s_rstd, done + b)
                nc.gpsimd.tensor_tensor(cut(var_eps, s, C), mv, ln_eps[:, :], ALU.add).then_inc(s_ve, 1)
                pool.wait_ge(s_ve, done + b + 1)
                nc.gpsimd.tensor_tensor(cut(rstd, s, C), cut(var_eps, s, C), minus_half[:, :],
                                        ALU.pow).then_inc(s_rstd, 1)
            return turn

        def statistics(src, s):
            for c in range(C):
                nc.vector.bn_stats(cut(stats, s, C * 6, c * 6, 6), src[:, c]).then_inc(s_stats, 1)

        def means(s):
            for c in range(C):
                nc.vector.bn_aggr(cut(mean_var, s, C * 2, c * 2, 2),
                                  cut(stats, s, C * 6, c * 6, 6)).then_inc(s_mv, 1)

        def normed(dst, src, s, done):
            for c in range(C):
                nc.vector.tensor_scalar(dst[:, c], src[:, c], cut(mean_var, s, 2 * C, 2 * c, 1),
                                        cut(rstd, s, C, c, 1), ALU.subtract, ALU.mult).then_inc(done, 1)

        @block.sync
        def _(sp):
            step = B // XCH

            def load_x(n):
                sp.dma_start(x_sb[:, n * step * C * D:(n + 1) * step * C * D]
                             .rearrange("p (b k) -> p b k", b=step),
                             x[n * step:(n + 1) * step].rearrange("b (p c) d -> p b (c d)", p=P)
                             ).then_inc(s_x[n], 16)

            sp.dma_start(edges_row_i[:], edges_row[0].partition_broadcast(P)).then_inc(s_edges, 16)
            sp.dma_start(edges_col_i[:], edges_col).then_inc(s_edges, 16)
            load_x(0)
            sp.dma_start(nets_sb[:], nets).then_inc(s_nets, 16)
            sp.dma_start(a_sb[:], a_col).then_inc(s_nets, 16)
            sp.dma_start(adj_sb[:].rearrange("p (c m) -> p c m", c=C),
                         adj.rearrange("(p c) m -> p c m", p=P)).then_inc(s_adj, 16)
            for n in range(1, XCH):
                load_x(n)
            sp.dma_start(router_sb[:], router).then_inc(s_route_in, 16)
            sp.dma_start(br_sb[:], br.partition_broadcast(B)).then_inc(s_route_in, 16)
            sp.dma_start(b2_sb[:], b2).then_inc(s_route_in, 16)
            sp.dma_start(gamma_sb[:], gamma.partition_broadcast(P)).then_inc(s_route_in, 16)
            sp.dma_start(beta_sb[:], beta.partition_broadcast(P)).then_inc(s_route_in, 16)
            sp.dma_start(experts_sb[:], experts).then_inc(s_experts, 16)
            for n in range(XCH):
                sp.wait_ge(s_x[n], 16)
                sp.sem_inc(s_x_ready, step)
            with sp.Fori(0, B // 2) as j:
                sp.wait_ge(s_res, 2 * j + 2)
                sp.dma_start(out[bass.ds(2 * j, 2)].rearrange("b (p c) d -> p b (c d)", p=P),
                             x_sb[:, bass.ds(j * 2 * C * D, 2 * C * D)].rearrange("p (b k) -> p b k", b=2)
                             ).then_inc(s_out, 16)
            sp.wait_ge(s_out, 16 * (B // 2))

        @block.gpsimd
        def _(pool):
            nc.gpsimd.iota(count_row[:], [[1, N]], base=0, channel_multiplier=0,
                           allow_small_or_imprecise_dtypes=True).then_inc(s_const, 1)
            nc.gpsimd.iota(edge_col[:], [[P, K]], base=0, channel_multiplier=1,
                           allow_small_or_imprecise_dtypes=True).then_inc(s_const, 1)
            nc.gpsimd.iota(node_col[:], [[1, C]], base=0, channel_multiplier=C,
                           allow_small_or_imprecise_dtypes=True).then_inc(s_const, 1)
            nc.gpsimd.iota(node_row[:].rearrange("p (c n) -> p c n", c=C), [[1, C], [C, P]], base=0,
                           channel_multiplier=0, allow_small_or_imprecise_dtypes=True).then_inc(s_const, 1)
            nc.gpsimd.memset(ones[:], 1.0).then_inc(s_const, 1)
            nc.gpsimd.memset(minus_half[:], -0.5).then_inc(s_const, 1)
            nc.gpsimd.memset(ln_eps[:], LN_EPS).then_inc(s_const, 1)
            nc.gpsimd.memset(ident[:], 0.0).then_inc(s_ident, 1)
            pool.wait_ge(s_ident, 1)
            nc.gpsimd.affine_select(out=ident[:], in_=ident[:], compare_op=ALU.not_equal, fill=1.0, base=0,
                                    pattern=[[-1, P]], channel_multiplier=1).then_inc(s_ident, 1)
            pool.wait_ge(s_const, 7)
            turns(pool, 0, layer_norm_scale(pool, 0))
            turns(pool, 0, layer_norm_scale(pool, B))

            pool.wait_ge(s_route_in, 16 * 5)
            scale = layer_norm_scale(pool, 2 * B)

            def turn(i, r):
                if live(i):
                    scale(i, r)
                if live(i - 1):
                    b, s = i - 1, (r + 1) % 2
                    gamma_c = gamma_sb[:].unsqueeze(1).to_broadcast([P, C, D])
                    beta_c = beta_sb[:].unsqueeze(1).to_broadcast([P, C, D])
                    pool.wait_ge(s_yn, C * b + C)
                    if from_second(b):
                        pool.wait_ge(s_yb, b - 1)
                    nc.gpsimd.tensor_tensor(halves(cut(y_gamma, s, C * D)), halves(cut(y, s, C * D)),
                                            gamma_c, ALU.mult).then_inc(s_yg, 1)
                    pool.wait_ge(s_yg, b + 1)
                    if from_second(b):
                        pool.wait_ge(s_res, b - 1)
                    nc.gpsimd.tensor_tensor(halves(cut(y_beta, s, C * D)), halves(cut(y_gamma, s, C * D)),
                                            beta_c, ALU.add).then_inc(s_yb, 1)
            turns(pool, 1, turn)

        @block.scalar
        def _(act):
            nc.scalar.preload_act_table_set("natural_log_exp_and_others")
            act.wait_ge(s_prep, PREP_ADJ)
            nc.scalar.activation(log_adj[:], rank[:], ACT.Ln).then_inc(s_prep_act, 1)

            def turn(i, r):
                if live(i - 1):
                    b, s = i - 1, (r + 1) % 2
                    act.wait_ge(s_z, C * b + C)
                    if from_second(b):
                        act.wait_ge(s_G, b - 1)
                    nc.scalar.copy(cut(z_hi, s, C * D), cut(z, s, C * D)).then_inc(s_zhi, 1)
                if live(i - 2):
                    b, s = i - 2, r
                    act.wait_ge(s_G, b + 1)
                    if from_second(b):
                        act.wait_ge(s_vp, b - 1)
                    nc.scalar.copy(cut(gathered, s, 2 * E), banks[s][:]).then_inc(s_gt, 1)
                if live(i - 3):
                    b, s = i - 3, (r + 1) % 2
                    act.wait_ge(s_vp, b + 1)
                    if from_second(b):
                        act.wait_ge(s_lr, b - 1)
                    nc.scalar.mul(cut(q_low, s, E), banks[2 + s][:, 0:E], SLOPE).then_inc(s_qlow, 1)
                    nc.scalar.copy(cut(v_sb, b, K * D), banks[2 + s][:, E:E + K * D]).then_inc(s_vs, 1)
            turns(act, 3, turn)

            act.wait_ge(s_sm, SM_SHIFTED)
            nc.scalar.activation(expo[:], shifted[:], ACT.Exp).then_inc(s_sm_act, 1)

            def turn(i, r):
                if live(i):
                    b, s = i, r
                    act.wait_ge(s_av, b + 1)
                    if from_second(b):
                        act.wait_ge(s_y, b - 1)
                    nc.scalar.copy(cut(av_hi, s, K * D), cut(av, s, K * D)).then_inc(s_avhi, 1)
                if live(i - 1):
                    b, s = i - 1, (r + 1) % 2
                    act.wait_ge(s_y, b + 1)
                    if from_second(b):
                        act.wait_ge(s_o, b - 1)
                    nc.scalar.copy(cut(yT, s, N), banks[s][:, 0:N]).then_inc(s_ys, 1)
                if live(i - 4):
                    b, s = i - 4, r
                    act.wait_ge(s_t, b + 1)
                    nc.scalar.activation(cut(uT_sb, b, N), banks[4 + s][:, 0:N], ACT.Copy,
                                         accum_out=usum[:, bass.ds(b, 1)]).then_inc(s_ut, 1)
            turns(act, 4, turn)

            act.wait_ge(s_rt, RT_SHIFT1)
            nc.scalar.activation(route[:, 3 * X:4 * X], route[:, 2 * X:3 * X], ACT.Exp).then_inc(s_rt_act, 1)
            act.wait_ge(s_rt, RT_SHIFT2)
            nc.scalar.activation(route[:, 9 * X:10 * X], route[:, 8 * X:9 * X], ACT.Exp).then_inc(s_rt_act, 1)
            act.wait_ge(s_rt, RT_DIFF)
            nc.scalar.activation(small[:, 8:9], small[:, 7:8], ACT.Exp).then_inc(s_rt_act, 1)
            nc.scalar.preload_act_table(ACT.Gelu)

            def turn(i, r):
                b, s = i, r
                act.wait_ge(s_h, b + 1)
                if from_second(b):
                    act.wait_ge(s_f, b - 1)
                for k in range(TOP):
                    for c in range(FC):
                        nc.scalar.activation(
                            cut(hT, (s * TOP + k) * FC + c, N),
                            banks[2 * s + k][:, c * N:(c + 1) * N], ACT.Gelu,
                            bias=cut(chosen, s * TOP + k, EW, F + c, 1)).then_inc(s_gelu, 1)
            turns(act, 0, turn)

        @block.vector
        def _(dve):
            prep = [0]

            def chain(ins, s, n, hold=True):
                n[0] += 1
                ins.then_inc(s, 1)
                if hold:
                    dve.wait_ge(s, n[0])

            dve.wait_ge(s_edges, 32)
            dve.wait_ge(s_const, 7)
            chain(nc.vector.tensor_copy(edges_col_f[:], edges_col_i[:]), s_prep, prep)
            chain(nc.vector.scalar_tensor_tensor(out=key_row[:], in0=edges_row_i[:], scalar=float(E),
                                                 in1=count_row[:], op0=ALU.mult, op1=ALU.add),
                  s_prep, prep, False)
            chain(nc.vector.scalar_tensor_tensor(out=key_col[:], in0=edges_col_f[:, 0:K], scalar=float(E),
                                                 in1=edge_col[:], op0=ALU.mult, op1=ALU.add), s_prep, prep)
            for k in range(K):
                chain(nc.vector.tensor_scalar(cut(before, k, E), key_row[:], key_col[:, k:k + 1], None,
                                              ALU.is_lt), s_prep, prep, k == K - 1)
            chain(nc.vector.tensor_reduce(rank[:], before[:].rearrange("p (k e) -> p k e", k=K),
                                          AX.X, ALU.add), s_prep, prep)
            for k in range(K):
                chain(nc.vector.tensor_scalar(cut(place, k, E), count_row[:], rank[:, k:k + 1], None,
                                              ALU.is_equal), s_prep, prep, False)
                for q in range(2):
                    chain(nc.vector.tensor_scalar(cut(placed, 2 * k + q, E), count_row[:], rank[:, k:k + 1],
                                                  edges_col_f[:, q * K + k:q * K + k + 1],
                                                  ALU.is_equal, ALU.mult), s_prep, prep, False)
            assert prep[0] == PREP_PLACED
            dve.wait_ge(s_prep_pe, 2)
            chain(nc.vector.tensor_copy(sorted_row[:], banks[0][:]), s_prep, prep, False)
            chain(nc.vector.tensor_copy(sorted_col[:], banks[1][:, 0:2 * K]), s_prep, prep)
            for c in range(C):
                for q, hot in enumerate((source_of, target_of)):
                    chain(nc.vector.tensor_scalar(cut(hot, c, E), cut(sorted_row, q, E),
                                                  node_col[:, c:c + 1], None, ALU.is_equal),
                          s_prep, prep, (c, q) == (C - 1, 1))
            for c in range(C):
                chain(nc.vector.tensor_tensor(cut(gather, 2 * c, E), cut(source_of, c, E),
                                              cut(target_of, c, E), ALU.add), s_prep, prep, False)
                chain(nc.vector.tensor_copy(cut(gather, 2 * c + 1, E), cut(target_of, c, E)),
                      s_prep, prep, False)
            assert prep[0] == PREP_GATHER
            nc.vector.memset(a_heads[:], 0.0).then_inc(s_prep, 1)
            prep[0] += 1
            dve.wait_ge(s_nets, 32)
            dve.wait_ge(s_prep, prep[0])
            for h in range(H):
                chain(nc.vector.tensor_copy(a_heads[h * DH:(h + 1) * DH, h:h + 1],
                                            a_sb[h * DH:(h + 1) * DH, :]), s_prep, prep, False)
            for k in range(K):
                chain(nc.vector.tensor_scalar(cut(spread, k, N), node_row[:],
                                              sorted_col[:, 2 * k:2 * k + 1], None, ALU.is_equal),
                      s_prep, prep, False)
                chain(nc.vector.tensor_scalar(cut(target_hot, k, N), count_row[:],
                                              sorted_col[:, 2 * k + 1:2 * k + 2], None, ALU.is_equal),
                      s_prep, prep, k == K - 1)
            dve.wait_ge(s_prep_pe, 3)
            chain(nc.vector.tensor_tensor(adj_pick[:], banks[2][:], target_hot[:], ALU.mult), s_prep, prep)
            chain(nc.vector.tensor_reduce(rank[:], adj_pick[:].rearrange("p (k m) -> p k m", k=K),
                                          AX.X, ALU.add), s_prep, prep)
            chain(nc.vector.tensor_scalar(rank[:], rank[:], LOG_EPS, None, ALU.add), s_prep, prep, False)
            assert prep[0] == PREP_ADJ
            chain(nc.vector.memset(same[:], 0.0), s_prep, prep)
            chain(nc.vector.tensor_tensor(same[:, 1:E], sorted_row[:, 1:E], sorted_row[:, 0:E - 1],
                                          ALU.is_equal), s_prep, prep)
            chain(nc.vector.tensor_scalar(start_low[:], same[:, 0:E], -LOW, LOW, ALU.mult, ALU.add),
                  s_prep, prep, False)
            chain(nc.vector.tensor_scalar(is_last[:], same[:, 1:E + 1], -1.0, 1.0, ALU.mult, ALU.add),
                  s_prep, prep)

            def turn(i, r):
                if live(i):
                    dve.wait_ge(s_x_ready, i + 1)
                    if from_second(i):
                        dve.wait_ge(s_mv, C * (i - 1))
                if live(i - 1):
                    b, s = i - 1, (r + 1) % 2
                    dve.wait_ge(s_rstd, b + 1)
                    if from_second(b):
                        dve.wait_ge(s_zhi, b - 1)
                        dve.wait_ge(s_zlo, b - 1)
                    normed(halves(cut(z, s, C * D)), halves(cut(x_sb, b, C * D)), s, s_z)
                if live(i):
                    statistics(halves(cut(x_sb, i, C * D)), r)
                    dve.wait_ge(s_stats, C * i + C)
                    if from_second(i):
                        dve.wait_ge(s_z, C * (i - 1))
                if live(i - 1):
                    b, s = i - 1, (r + 1) % 2
                    dve.wait_ge(s_zhi, b + 1)
                    if from_second(b):
                        dve.wait_ge(s_G, b - 1)
                    nc.vector.tensor_tensor(cut(z_lo, s, C * D), cut(z, s, C * D),
                                            cut(z_hi, s, C * D).bitcast(f32), ALU.subtract).then_inc(s_zlo, 1)
                if live(i):
                    means(r)
                if live(i - 3):
                    b, s = i - 3, (r + 1) % 2
                    dve.wait_ge(s_vs, b + 1)
                    if from_second(b):
                        dve.wait_ge(s_e, b - 1)
                    nc.vector.tensor_tensor(cut(act_q, s, E), banks[2 + s][:, 0:E], cut(q_low, s, E),
                                            ALU.max).then_inc(s_lr, 1)
            turns(dve, 3, turn)

            sm = [0]
            dve.wait_ge(s_e, B)
            dve.wait_ge(s_prep_act, 1)
            for k in range(K):
                chain(nc.vector.tensor_scalar(
                    cut(logits_e, k, ROWS).rearrange("p (b h) -> p b h", h=H),
                    banks[4][:, 0:B * K * H].rearrange("p (b k h) -> p k b h", k=K, h=H)[:, k],
                    log_adj[:, k:k + 1], None, ALU.add), s_sm, sm, False)
            assert sm[0] == SM_LOGITS
            dve.wait_ge(s_sm_pe, 1)
            chain(nc.vector.tensor_copy(logits[:], banks[5][0:ROWS, 0:E]), s_sm, sm)
            chain(nc.vector.tensor_tensor_scan(scan[:], start_low[0:ROWS], logits[:], LOW, ALU.add, ALU.max),
                  s_sm, sm)
            chain(nc.vector.tensor_tensor(at_last[:], scan[:], is_last[0:ROWS], ALU.mult), s_sm, sm)
            chain(nc.vector.tensor_tensor_scan(seg_max[:, ::-1], same[0:ROWS, E:0:-1], at_last[:, ::-1], 0.0,
                                               ALU.mult, ALU.add), s_sm, sm)
            chain(nc.vector.tensor_tensor(shifted[:], logits[:], seg_max[:], ALU.subtract), s_sm, sm, False)
            assert sm[0] == SM_SHIFTED
            dve.wait_ge(s_sm_act, 1)
            chain(nc.vector.tensor_tensor_scan(scan[:], same[0:ROWS, 0:E], expo[:], 0.0, ALU.mult, ALU.add),
                  s_sm, sm)
            chain(nc.vector.tensor_tensor(at_last[:], scan[:], is_last[0:ROWS], ALU.mult), s_sm, sm)
            chain(nc.vector.tensor_tensor_scan(seg_sum[:, ::-1], same[0:ROWS, E:0:-1], at_last[:, ::-1], 0.0,
                                               ALU.mult, ALU.add), s_sm, sm)
            chain(nc.vector.reciprocal(scan[:], seg_sum[:]), s_sm, sm)
            chain(nc.vector.tensor_tensor(attn[:], expo[:], scan[:], ALU.mult), s_sm, sm, False)
            assert sm[0] == SM_ATTN
            dve.wait_ge(s_sm_pe, 2)
            chain(nc.vector.tensor_copy(attn_e[:], banks[5][:, 0:K * ROWS]), s_sm, sm)

            def turn(i, r):
                if live(i - 2):
                    b, s = i - 2, r
                    xb = cut(x_sb, b, C * D)
                    dve.wait_ge(s_o, b + 1)
                    nc.vector.tensor_tensor(xb, banks[2 + s][:, 0:C * D], xb, ALU.add).then_inc(s_x1, 1)
                    dve.wait_ge(s_x1, b + 1)
                    dve.wait_ge(s_mv, C * (B + b - 1))
                if live(i):
                    if from_second(i):
                        dve.wait_ge(s_avhi, i - 1)
                        dve.wait_ge(s_avlo, i - 1)
                    weights = attn_e[:].rearrange("p (k b h) -> p b k h", k=K, h=H)[:, bass.ds(i, 1)]
                    weights = weights.rearrange("p b k h -> p (b k) h").unsqueeze(3)
                    nc.vector.tensor_tensor(
                        cut(av, r, K * D).rearrange("p (k h d) -> p k h d", k=K, h=H),
                        cut(v_sb, i, K * D).rearrange("p (k h d) -> p k h d", k=K, h=H),
                        weights.to_broadcast([P, K, H, DH]), ALU.mult).then_inc(s_av, 1)
                if live(i - 2):
                    b, s = i - 2, r
                    statistics(halves(cut(x_sb, b, C * D)), s)
                    dve.wait_ge(s_stats, C * (B + b) + C)
                    if from_second(b):
                        dve.wait_ge(s_u, C * (b - 1))
                if live(i):
                    dve.wait_ge(s_avhi, i + 1)
                    if from_second(i):
                        dve.wait_ge(s_y, i - 1)
                    nc.vector.tensor_tensor(cut(av_lo, r, K * D), cut(av, r, K * D),
                                            cut(av_hi, r, K * D).bitcast(f32), ALU.subtract).then_inc(s_avlo, 1)
                if live(i - 2):
                    means(r)
                if live(i - 3):
                    b, s = i - 3, (r + 1) % 2
                    dve.wait_ge(s_rstd, B + b + 1)
                    if from_second(b):
                        dve.wait_ge(s_t, b - 1)
                    normed(halves(cut(u, s, C * D)), halves(cut(x_sb, b, C * D)), s, s_u)
            turns(dve, 3, turn)

            rt = [0]

            def col(n):
                return route[:, n * X:(n + 1) * X]

            def softmax(at, out_at, src, n_act):
                chain(nc.vector.tensor_reduce(small[:, at:at + 1], src, AX.X, ALU.max), s_rt, rt)
                chain(nc.vector.tensor_scalar(col(out_at), src, small[:, at:at + 1], None, ALU.subtract),
                      s_rt, rt, False)
                dve.wait_ge(s_rt_act, n_act)
                chain(nc.vector.tensor_reduce(small[:, at + 1:at + 2], col(out_at + 1), AX.X, ALU.add), s_rt, rt)
                chain(nc.vector.reciprocal(small[:, at + 2:at + 3], small[:, at + 1:at + 2]), s_rt, rt)
                chain(nc.vector.tensor_scalar(col(out_at + 2), col(out_at + 1), small[:, at + 2:at + 3], None,
                                              ALU.mult), s_rt, rt)

            dve.wait_ge(s_route_in, 16 * 5)
            dve.wait_ge(s_rt_pe, 1)
            chain(nc.vector.scalar_tensor_tensor(out=col(1), in0=banks[6][0:B, 0:X], scalar=1.0 / N,
                                                 in1=br_sb[:], op0=ALU.mult, op1=ALU.add), s_rt, rt)
            softmax(0, 2, col(1), 1)
            assert rt[0] == RT_PROBS
            dve.wait_ge(s_rt_pe, 2)
            chain(nc.vector.tensor_scalar(col(5), banks[7][0:B, 0:X], float(N), None, ALU.mult), s_rt, rt)
            chain(nc.vector.reciprocal(col(6), col(5)), s_rt, rt)
            chain(nc.vector.tensor_scalar(col(6), col(6), CAPACITY, 1.0, ALU.mult, ALU.min), s_rt, rt)
            chain(nc.vector.tensor_tensor(col(7), col(4), col(6), ALU.mult), s_rt, rt)
            softmax(3, 8, col(7), 2)
            chain(nc.vector.max(col(11), col(10)), s_rt, rt)
            chain(nc.vector.max_index(top_i[:], col(11), col(10)), s_rt, rt)
            chain(nc.vector.tensor_tensor(small[:, 7:8], route[:, 11 * X + 1:11 * X + 2],
                                          route[:, 11 * X:11 * X + 1], ALU.subtract), s_rt, rt, False)
            assert rt[0] == RT_DIFF
            chain(nc.vector.tensor_copy(col(12), top_i[:]), s_rt, rt)
            dve.wait_ge(s_rt_act, 3)
            chain(nc.vector.tensor_scalar(small[:, 9:10], small[:, 8:9], 1.0, None, ALU.add), s_rt, rt)
            chain(nc.vector.reciprocal(small[:, 10:11], small[:, 9:10]), s_rt, rt)
            chain(nc.vector.tensor_tensor(small[:, 11:12], small[:, 10:11], small[:, 8:9], ALU.mult), s_rt, rt)
            chain(nc.vector.tensor_scalar(small[:, 12:12 + TOP], route[:, 12 * X:12 * X + TOP], float(EW), None,
                                          ALU.mult), s_rt, rt)
            chain(nc.vector.tensor_tensor(
                spread_w[:].rearrange("p (b q) -> p b q", q=2 * TOP),
                ident[0:B, 0:B].unsqueeze(2).to_broadcast([B, B, 2 * TOP]),
                small[:, 10:10 + 2 * TOP].unsqueeze(1).to_broadcast([B, B, 2 * TOP]), ALU.mult),
                s_rt, rt, False)
            for k in range(TOP):
                chain(nc.vector.tensor_scalar(col(13 + k), count_row[0:B, 0:X],
                                              route[:, 12 * X + k:12 * X + k + 1], small[:, 10 + k:11 + k],
                                              ALU.is_equal, ALU.mult), s_rt, rt, k == TOP - 1)
            chain(nc.vector.tensor_tensor(col(15), col(13), col(14), ALU.add), s_rt, rt, False)
            assert rt[0] == RT_DENSE
            dve.wait_ge(s_rt_pe, 4)
            chain(nc.vector.tensor_copy(dense_wT[:], banks[6][0:X, 0:B]), s_rt, rt, False)
            chain(nc.vector.tensor_copy(weight_bc[:], banks[7][:, 0:B * 2 * TOP]), s_rt, rt)
            chain(nc.vector.tensor_copy(offsets_i[:], weight_bc[:]), s_rt, rt)
            assert rt[0] == RT_TURNED
            dve.wait_ge(s_rt_pe, 5)
            chain(nc.vector.tensor_copy(b2_mix[:], banks[6][:, 0:B]), s_rt, rt)

            dve.wait_ge(s_experts, 16)
            top_off = (X - 1) * EW

            def turn(i, r):
                if live(i):
                    if from_second(i):
                        dve.wait_ge(s_f, i - 1)
                    for k in range(TOP):
                        off = nc.vector.value_load(offsets_i[0:1, bass.ds(i * 2 * TOP + TOP + k, 1)],
                                                   min_val=0, max_val=top_off)
                        nc.vector.tensor_copy(cut(chosen, r * TOP + k, EW, 0, F + FC),
                                              experts_sb[:, bass.ds(off, F + FC)]).then_inc(s_sel, 1)
                        nc.vector.tensor_scalar(cut(chosen, r * TOP + k, EW, F + FC, FC * D),
                                                experts_sb[:, bass.ds(off + F + FC, FC * D)],
                                                weight_bc[:, bass.ds(i * 2 * TOP + k, 1)], None,
                                                ALU.mult).then_inc(s_sel, 1)
                if live(i - 3):
                    b = i - 3
                    dve.wait_ge(s_tr, b + 1)
                    dve.wait_ge(s_mv, C * (2 * B + b - 1))
                if live(i - 2):
                    b, s = i - 2, r
                    dve.wait_ge(s_f, b + 1)
                    if from_second(b):
                        dve.wait_ge(s_tr, b - 1)
                    nc.vector.scalar_tensor_tensor(out=cut(sT, s, N), in0=banks[4 + s][:, 0:N],
                                                   scalar=b2_mix[:, bass.ds(b, 1)], in1=cut(uT_sb, b, N),
                                                   op0=ALU.add, op1=ALU.add).then_inc(s_s, 1)
                if live(i - 3):
                    b, s = i - 3, (r + 1) % 2
                    statistics(halves(banks[6 + s][:, 0:C * D]), s)
                    dve.wait_ge(s_stats, C * (2 * B + b) + C)
                    if from_second(b):
                        dve.wait_ge(s_yn, C * (b - 1))
                if live(i - 4):
                    b, s = i - 4, r
                    dve.wait_ge(s_rstd, 2 * B + b + 1)
                    if from_second(b):
                        dve.wait_ge(s_yg, b - 1)
                    normed(halves(cut(y, s, C * D)), halves(banks[6 + s][:, 0:C * D]), s, s_yn)
                if live(i - 3):
                    means((r + 1) % 2)
                if live(i - 5):
                    b, s = i - 5, (r + 1) % 2
                    xb = cut(x_sb, b, C * D)
                    dve.wait_ge(s_yb, b + 1)
                    nc.vector.tensor_tensor(xb, cut(y_beta, s, C * D), xb, ALU.add).then_inc(s_res, 1)
            turns(dve, 5, turn)

        @block.tensor
        def _(pe):
            def mm(out_, lhsT, rhs, start=True, stop=True):
                return nc.tensor.matmul(out_, lhsT, rhs, start=start, stop=stop)

            pe.wait_ge(s_prep, PREP_PLACED)
            pe.wait_ge(s_const, 7)
            for k in range(K):
                last = mm(banks[0][:], ones[:], cut(placed, k, 2 * E), k == 0, k == K - 1)
            last.then_inc(s_prep_pe, 1)
            for j in range(K):
                for k in range(K):
                    last = mm(banks[1][:, 2 * j:2 * j + 2], cut(place, k, E, j * P, P),
                              edges_col_f[:].rearrange("p (q k) -> p k q", k=K)[:, k], k == 0, k == K - 1)
            last.then_inc(s_prep_pe, 1)
            pe.wait_ge(s_prep, PREP_GATHER)
            pe.wait_ge(s_adj, 16)
            for k in range(K):
                for c in range(C):
                    last = mm(banks[2][:, k * N:(k + 1) * N], cut(source_of, c, E, k * P, P),
                              cut(adj_sb, c, N), c == 0, c == C - 1)
            last.then_inc(s_prep_pe, 1)
            pe.wait_ge(s_prep, PREP_ADJ)

            def turn(i, r):
                if live(i - 1):
                    b, s = i - 1, (r + 1) % 2
                    pe.wait_ge(s_zlo, b + 1)
                    if from_second(b):
                        pe.wait_ge(s_gt, b - 1)
                    for c in range(C):
                        for part in (z_hi, z_lo):
                            last = mm(banks[s][:], cut(part, s * C + c, D), cut(gather, c, 2 * E),
                                      c == 0 and part is z_hi, c == C - 1 and part is z_lo)
                    last.then_inc(s_G, 1)
                if live(i - 2):
                    b, s = i - 2, r
                    pe.wait_ge(s_gt, b + 1)
                    if from_second(b):
                        pe.wait_ge(s_lr, b - 1)
                    mm(banks[2 + s][:, 0:E], W_LIN, cut(gathered, s, 2 * E, 0, E))
                    for k in range(K):
                        last = mm(banks[2 + s][:, E + k * D:E + (k + 1) * D],
                                  cut(gathered, s, 2 * E, E + k * P, P), W_VAL)
                    last.then_inc(s_vp, 1)
                if live(i - 3):
                    b, s = i - 3, (r + 1) % 2
                    pe.wait_ge(s_lr, b + 1)
                    for k in range(K):
                        last = mm(banks[4][:, bass.ds(b * K * H + k * H, H)], cut(act_q, s, E, k * P, P),
                                  a_heads[:])
                    last.then_inc(s_e, 1)
            turns(pe, 3, turn)

            pe.wait_ge(s_ident, 2)
            pe.wait_ge(s_sm, SM_LOGITS)
            for k in range(K):
                last = nc.tensor.transpose(banks[5][0:ROWS, k * P:(k + 1) * P], cut(logits_e, k, ROWS), ident[:])
            last.then_inc(s_sm_pe, 1)
            pe.wait_ge(s_sm, SM_ATTN)
            for k in range(K):
                last = nc.tensor.transpose(banks[5][:, k * ROWS:(k + 1) * ROWS], attn[:, k * P:(k + 1) * P],
                                           ident[0:ROWS, 0:ROWS])
            last.then_inc(s_sm_pe, 1)

            def turn(i, r):
                if live(i):
                    b, s = i, r
                    pe.wait_ge(s_avlo, b + 1)
                    if from_second(b):
                        pe.wait_ge(s_ys, b - 1)
                    for k in range(K):
                        for part in (av_hi, av_lo):
                            last = mm(banks[s][:, 0:N], cut(part, s * K + k, D), cut(spread, k, N),
                                      k == 0 and part is av_hi, k == K - 1 and part is av_lo)
                    last.then_inc(s_y, 1)
                if live(i - 1):
                    b, s = i - 1, (r + 1) % 2
                    pe.wait_ge(s_ys, b + 1)
                    if from_second(b):
                        pe.wait_ge(s_x1, b - 1)
                    for c in range(C):
                        last = mm(banks[2 + s][:, c * D:(c + 1) * D], cut(yT, s, N, c * P, P), W_OUT)
                    last.then_inc(s_o, 1)
                if live(i - 3):
                    b, s = i - 3, (r + 1) % 2
                    pe.wait_ge(s_u, C * b + C)
                    if from_second(b):
                        pe.wait_ge(s_ut, b - 1)
                    for c in range(C):
                        last = nc.tensor.transpose(banks[4 + s][:, c * P:(c + 1) * P],
                                                   cut(u, s * C + c, D), ident[:])
                    last.then_inc(s_t, 1)
            turns(pe, 3, turn)

            pe.wait_ge(s_route_in, 16 * 5)
            pe.wait_ge(s_ut, B)
            mm(banks[6][0:B, 0:X], usum[:], router_sb[:]).then_inc(s_rt_pe, 1)
            pe.wait_ge(s_rt, RT_PROBS)
            mm(banks[7][0:B, 0:X], ones[0:B, 0:B], route[:, 4 * X:5 * X]).then_inc(s_rt_pe, 1)
            pe.wait_ge(s_rt, RT_DENSE)
            nc.tensor.transpose(banks[6][0:X, 0:B], route[:, 15 * X:16 * X], ident[0:B, 0:B]).then_inc(s_rt_pe, 1)
            mm(banks[7][:, 0:B * 2 * TOP], ones[0:B, :], spread_w[:]).then_inc(s_rt_pe, 1)
            pe.wait_ge(s_rt, RT_TURNED)
            mm(banks[6][:, 0:B], b2_sb[:], dense_wT[:]).then_inc(s_rt_pe, 1)
            pe.wait_ge(s_rt, RT_TURNED + 1)

            def turn(i, r):
                if live(i):
                    b, s = i, r
                    pe.wait_ge(s_sel, 2 * TOP * (b + 1))
                    if from_second(b):
                        pe.wait_ge(s_gelu, TOP * FC * (b - 1))
                    for k in range(TOP):
                        for c in range(FC):
                            last = mm(banks[2 * s + k][:, c * N:(c + 1) * N],
                                      cut(chosen, s * TOP + k, EW, c * P, P), cut(uT_sb, b, N))
                    last.then_inc(s_h, 1)
                if live(i - 1):
                    b, s = i - 1, (r + 1) % 2
                    pe.wait_ge(s_gelu, TOP * FC * (b + 1))
                    if from_second(b):
                        pe.wait_ge(s_s, b - 1)
                    for k in range(TOP):
                        for c in range(FC):
                            last = mm(banks[4 + s][:, 0:N],
                                      cut(chosen, s * TOP + k, EW, F + FC + c * D, D),
                                      cut(hT, (s * TOP + k) * FC + c, N),
                                      k == 0 and c == 0, k == TOP - 1 and c == FC - 1)
                    last.then_inc(s_f, 1)
                if live(i - 2):
                    b, s = i - 2, r
                    pe.wait_ge(s_s, b + 1)
                    if from_second(b):
                        pe.wait_ge(s_yn, C * (b - 1))
                    for c in range(C):
                        last = nc.tensor.transpose(banks[6 + s][:, c * P:(c + 1) * P],
                                                   cut(sT, s, N, c * P, P), ident[:])
                    last.then_inc(s_tr, 1)
            turns(pe, 2, turn)


PREP_PLACED = 12
PREP_GATHER = 22
PREP_ADJ = 34
SM_LOGITS = 2
SM_SHIFTED = 7
SM_ATTN = 12
RT_SHIFT1 = 3
RT_PROBS = 6
RT_SHIFT2 = 12
RT_DIFF = 18
RT_DENSE = 27
RT_TURNED = 30


def kernel(**inputs):
    import numpy as np
    import concourse.bacc as bacc
    from concourse import mybir
    from concourse.bass_utils import run_bass_kernel_spmd

    get = {k: np.asarray(v) for k, v in inputs.items()}
    P = 128
    W1, b1, W2 = get["L0_ffn_W1"], get["L0_ffn_b1"], get["L0_ffn_W2"]
    X, D, F = W1.shape
    src, dst = get["L0_gnn_src"], get["L0_gnn_dst"]
    K = src.shape[0] // P
    arrays = {
        "x": get["x"],
        "adj": get["adj"],
        "nets": np.concatenate([get["L0_gnn_W_lin"].T, get["L0_gnn_W_val"].T, get["L0_gnn_W_out"].T], axis=1),
        "a_col": get["L0_gnn_a"].reshape(D, 1),
        "router": get["L0_ffn_Wr"],
        "experts": np.concatenate([W1.transpose(1, 0, 2), b1.reshape(X, F // P, P).transpose(2, 0, 1),
                                   W2.reshape(X, F // P, P, D).transpose(2, 0, 1, 3).reshape(P, X, -1)],
                                  axis=2).reshape(P, -1),
        "edges_row": src.reshape(1, -1),
        "edges_col": np.concatenate([src.reshape(K, P).T, dst.reshape(K, P).T], axis=1),
        "br": get["L0_ffn_br"],
        "b2": get["L0_ffn_b2"],
        "gamma": get["L0_ffn_gamma"],
        "beta": get["L0_ffn_beta"],
    }
    nc = bacc.Bacc("TRN2", target_bir_lowering=False, num_devices=1)
    given, args = {}, []
    for name, a in arrays.items():
        a = np.ascontiguousarray(a)
        given[f"in_{name}"] = a
        args.append(nc.dram_tensor(f"in_{name}", a.shape, mybir.dt.from_np(a.dtype), kind="ExternalInput").ap())
    args.append(nc.dram_tensor("out_y", get["x"].shape, mybir.dt.float32, kind="ExternalOutput").ap())
    gnn_moe_program(nc, *args)
    r = run_bass_kernel_spmd(nc, [given], core_ids=[0])
    return r.results[0]["out_y"]
```

```python
import concourse.bass as bass
from concourse import mybir
from contextlib import ExitStack


def gnn_moe_program(nc, x, adj, nets, a_col, router, experts, edges_row, edges_col, br, b2, gamma, beta, out):
    f32 = mybir.dt.float32
    f32r = mybir.dt.float32r
    i32 = mybir.dt.int32
    u32 = mybir.dt.uint32
    ALU = mybir.AluOpType
    ACT = mybir.ActivationFunctionType
    AX = mybir.AxisListType

    P = 128
    B, N, D = x.shape
    C = N // P
    E = edges_row.shape[1]
    K = E // P
    H = 4
    DH = D // H
    X = br.shape[0]
    F = (experts.shape[1] // X) // 2 // P * P
    FC = F // P
    EW = F + FC + FC * D
    TOP = 2
    ROWS = B * H
    G = 2
    NP = B // G
    T = G * C
    CAPACITY = float(-(-B * N * 5 // 4 // X))
    SLOPE = 0.2
    LN_EPS = 1e-5
    LOG_EPS = 1e-8
    LOW = -1e30

    ctx = ExitStack()
    with ctx:
        def sb(name, shape, dt=f32):
            return ctx.enter_context(nc.sbuf_tensor(name, shape, dt))

        def sem(name):
            return ctx.enter_context(nc.semaphore(name))

        x_sb = sb("x_sb", [P, B * N // P * D])
        v_sb = sb("v_sb", [P, B * K * D])
        uT_sb = v_sb
        nets_sb = sb("nets_sb", [P, 3 * D])
        experts_sb = sb("experts_sb", [P, X * EW])
        gamma_sb = sb("gamma_sb", [P, D])
        beta_sb = sb("beta_sb", [P, D])
        router_sb = sb("router_sb", [P, X])
        br_sb = sb("br_sb", [B, X])
        b2_sb = sb("b2_sb", [X, D])
        adj_sb = sb("adj_sb", [P, C * N])
        a_sb = sb("a_sb", [P, 1])
        a_heads = sb("a_heads", [P, H])
        ident = sb("ident", [P, P])
        ones = sb("ones", [P, P])
        minus_half = sb("minus_half", [P, T])
        ln_eps = sb("ln_eps", [P, T])
        usum = sb("usum", [P, B])

        edges_row_i = sb("edges_row_i", [P, E], i32)
        edges_col_i = sb("edges_col_i", [P, 2 * K], i32)
        edges_col_f = sb("edges_col_f", [P, 2 * K])
        count_row = sb("count_row", [P, N])
        node_row = sb("node_row", [P, N])
        node_col = sb("node_col", [P, C])
        edge_col = sb("edge_col", [P, K])
        key_row = sb("key_row", [P, E])
        key_col = sb("key_col", [P, K])
        before = sb("before", [P, K * E])
        rank = sb("rank", [P, K])
        place = sb("place", [P, K * E])
        placed = sb("placed", [P, K * 2 * E])
        sorted_row = sb("sorted_row", [P, 2 * E])
        sorted_col = sb("sorted_col", [P, K * 2])
        source_of = sb("source_of", [P, C * E])
        target_of = sb("target_of", [P, C * E])
        gather = sb("gather", [P, C * 2 * E], f32r)
        spread = sb("spread", [P, K * N])
        target_hot = sb("target_hot", [P, K * N])
        adj_pick = sb("adj_pick", [P, K * N])
        log_adj = sb("log_adj", [P, K])
        same = sb("same", [P, E + 1])
        start_low = sb("start_low", [P, E])
        is_last = sb("is_last", [P, E])

        stats = sb("stats", [P, 2 * T * 6])
        mean_var = sb("mean_var", [P, 2 * T * 2])
        var_eps = sb("var_eps", [P, 2 * T])
        rstd = sb("rstd", [P, 2 * T])
        shift = sb("shift", [P, 2 * C])
        z = sb("z", [P, 2 * T * D])
        z_hi = sb("z_hi", [P, 2 * T * D], f32r)
        z_lo = sb("z_lo", [P, 2 * T * D], f32r)
        gathered = sb("gathered", [P, 2 * G * 2 * E])
        q_low = sb("q_low", [P, 2 * G * E])
        act_q = sb("act_q", [P, 2 * G * E])
        av = sb("av", [P, 2 * G * K * D])
        yT = sb("yT", [P, 2 * G * N])
        u = sb("u", [P, 2 * T * D])

        logits_e = sb("logits_e", [P, K * ROWS])
        logits = sb("logits", [ROWS, E])
        scan = sb("scan", [ROWS, E])
        at_last = sb("at_last", [ROWS, E])
        seg_max = sb("seg_max", [ROWS, E])
        shifted = sb("shifted", [ROWS, E])
        expo = sb("expo", [ROWS, E])
        seg_sum = sb("seg_sum", [ROWS, E])
        attn = sb("attn", [ROWS, E])
        attn_e = sb("attn_e", [P, K * ROWS])

        route = sb("route", [B, 24 * X])
        top_i = sb("top_i", [B, 8], u32)
        small = sb("small", [B, 16])
        spread_w = sb("spread_w", [B, B * 2 * TOP])
        dense_wT = sb("dense_wT", [X, B])
        weight_bc = sb("weight_bc", [P, B * 2 * TOP])
        offsets_i = sb("offsets_i", [P, B * TOP], i32)
        b2_mix = sb("b2_mix", [P, B])

        w1_sel = sb("w1_sel", [P, 2 * G * TOP * (F + FC)])
        w2_sel = sb("w2_sel", [P, 2 * G * TOP * FC * D])
        hT = sb("hT", [P, 2 * G * TOP * FC * N])
        sT = sb("sT", [P, 2 * G * N])
        y = z
        y_gamma = q_low
        y_beta = act_q

        psum = ctx.enter_context(nc.psum_tensor("psum", [P, 8 * 512], f32))
        banks = [psum[:, n * 512:(n + 1) * 512] for n in range(8)]

        XCH = 8
        s_edges, s_nets, s_adj, s_route_in, s_experts = (sem(n) for n in (
            "s_edges", "s_nets", "s_adj", "s_route_in", "s_experts"))
        s_x = [sem(f"s_x_in{n}") for n in range(XCH)]
        s_const, s_ident, s_prep, s_prep_pe, s_prep_act = (sem(n) for n in (
            "s_const", "s_ident", "s_prep", "s_prep_pe", "s_prep_act"))
        s_stats, s_mv, s_ve, s_rstd, s_z, s_zhi, s_zlo, s_G, s_gt, s_vp, s_vs, s_lr, s_e = (
            sem(n) for n in ("s_stats", "s_mv", "s_ve", "s_rstd", "s_z", "s_zhi", "s_zlo", "s_G", "s_gt",
                             "s_vp", "s_vs", "s_lr", "s_e"))
        s_sm, s_sm_pe, s_sm_act = sem("s_sm"), sem("s_sm_pe"), sem("s_sm_act")
        s_av, s_y, s_ys, s_o, s_x1, s_shift, s_u_dve, s_u_act, s_t, s_ut = (
            sem(n) for n in ("s_av", "s_y", "s_ys", "s_o", "s_x1", "s_shift", "s_u_dve", "s_u_act", "s_t", "s_ut"))
        s_rt, s_rt_pe, s_rt_act = sem("s_rt"), sem("s_rt_pe"), sem("s_rt_act")
        s_w1, s_w2, s_h, s_gelu, s_f, s_s, s_tr, s_yn, s_yg, s_yb, s_res, s_out = (
            sem(n) for n in ("s_w1", "s_w2", "s_h", "s_gelu", "s_f", "s_s", "s_tr", "s_yn", "s_yg", "s_yb",
                             "s_res", "s_out"))

        block = ctx.enter_context(nc.Block())

        def live(n):
            return not isinstance(n, int) or 0 <= n < NP

        def turns(eng, lag, turn):
            head = max(lag + lag % 2, 2)
            for i in range(head):
                turn(i, i % 2)
            with eng.Fori(head // 2, NP // 2) as j:
                turn(2 * j, 0)
                turn(2 * j + 1, 1)
            for i in range(NP, NP + lag):
                turn(i, i % 2)

        def cut(t, b, width, at=0, n=None):
            return t[:, bass.ds(b * width + at, width if n is None else n)]

        W_LIN, W_VAL, W_OUT = (nets_sb[:, n * D:(n + 1) * D] for n in range(3))

        def layer_norm_scale(pool, n, s, done):
            var = cut(mean_var, s, 2 * T).rearrange("p (t k) -> p t k", k=2)[:, :, 1]
            nc.gpsimd.tensor_tensor(cut(var_eps, s, T), var, ln_eps[:, :], ALU.add).then_inc(s_ve, 1)
            pool.wait_ge(s_ve, done + n + 1)
            nc.gpsimd.tensor_tensor(cut(rstd, s, T), cut(var_eps, s, T), minus_half[:, :],
                                    ALU.pow).then_inc(s_rstd, 1)

        def statistics(src, s):
            for t in range(T):
                last = nc.vector.bn_stats(cut(stats, s, T * 6, t * 6, 6), src[:, t * D:(t + 1) * D])
            last.then_inc(s_stats, 1)

        def means(s):
            for t in range(T):
                last = nc.vector.bn_aggr(cut(mean_var, s, T * 2, t * 2, 2), cut(stats, s, T * 6, t * 6, 6))
            last.then_inc(s_mv, 1)

        def normed(dst, src, s, slots, done):
            for t in slots:
                last = nc.vector.tensor_scalar(dst[:, t * D:(t + 1) * D], src[:, t * D:(t + 1) * D],
                                               cut(mean_var, s, 2 * T, 2 * t, 1), cut(rstd, s, T, t, 1),
                                               ALU.subtract, ALU.mult)
            last.then_inc(done, 1)

        @block.sync
        def _(sp):
            step = B // XCH

            def load_x(n):
                sp.dma_start(x_sb[:, n * step * C * D:(n + 1) * step * C * D]
                             .rearrange("p (b k) -> p b k", b=step),
                             x[n * step:(n + 1) * step].rearrange("b (p c) d -> p b (c d)", p=P)
                             ).then_inc(s_x[n], 16)

            sp.dma_start(edges_row_i[:], edges_row[0].partition_broadcast(P)).then_inc(s_edges, 16)
            sp.dma_start(edges_col_i[:], edges_col).then_inc(s_edges, 16)
            load_x(0)
            sp.dma_start(nets_sb[:], nets).then_inc(s_nets, 16)
            sp.dma_start(a_sb[:], a_col).then_inc(s_nets, 16)
            sp.dma_start(adj_sb[:].rearrange("p (c m) -> p c m", c=C),
                         adj.rearrange("(p c) m -> p c m", p=P)).then_inc(s_adj, 16)
            for n in range(1, XCH):
                load_x(n)
            sp.dma_start(router_sb[:], router).then_inc(s_route_in, 16)
            sp.dma_start(br_sb[:], br.partition_broadcast(B)).then_inc(s_route_in, 16)
            sp.dma_start(b2_sb[:], b2).then_inc(s_route_in, 16)
            sp.dma_start(gamma_sb[:], gamma.partition_broadcast(P)).then_inc(s_route_in, 16)
            sp.dma_start(beta_sb[:], beta.partition_broadcast(P)).then_inc(s_route_in, 16)
            sp.dma_start(experts_sb[:], experts).then_inc(s_experts, 16)
            with sp.Fori(0, NP) as n:
                sp.wait_ge(s_res, n + 1)
                sp.dma_start(out[bass.ds(n * G, G)].rearrange("b (p c) d -> p b (c d)", p=P),
                             cut(x_sb, n, T * D).rearrange("p (b k) -> p b k", b=G)).then_inc(s_out, 16)
            sp.wait_ge(s_out, 16 * NP)

        @block.gpsimd
        def _(pool):
            nc.gpsimd.iota(count_row[:], [[1, N]], base=0, channel_multiplier=0,
                           allow_small_or_imprecise_dtypes=True).then_inc(s_const, 1)
            nc.gpsimd.iota(edge_col[:], [[P, K]], base=0, channel_multiplier=1,
                           allow_small_or_imprecise_dtypes=True).then_inc(s_const, 1)
            nc.gpsimd.iota(node_col[:], [[1, C]], base=0, channel_multiplier=C,
                           allow_small_or_imprecise_dtypes=True).then_inc(s_const, 1)
            nc.gpsimd.iota(node_row[:].rearrange("p (c n) -> p c n", c=C), [[1, C], [C, P]], base=0,
                           channel_multiplier=0, allow_small_or_imprecise_dtypes=True).then_inc(s_const, 1)
            nc.gpsimd.memset(ones[:], 1.0).then_inc(s_const, 1)
            nc.gpsimd.memset(minus_half[:], -0.5).then_inc(s_const, 1)
            nc.gpsimd.memset(ln_eps[:], LN_EPS).then_inc(s_const, 1)
            nc.gpsimd.memset(ident[:], 0.0).then_inc(s_ident, 1)
            pool.wait_ge(s_ident, 1)
            nc.gpsimd.affine_select(out=ident[:], in_=ident[:], compare_op=ALU.not_equal, fill=1.0, base=0,
                                    pattern=[[-1, P]], channel_multiplier=1).then_inc(s_ident, 1)
            pool.wait_ge(s_const, 7)

            def turn(n, s):
                pool.wait_ge(s_mv, n + 1)
                layer_norm_scale(pool, n, s, 0)
            turns(pool, 0, turn)

            def turn(n, s):
                pool.wait_ge(s_mv, NP + n + 1)
                if not isinstance(n, int) or n >= 2:
                    pool.wait_ge(s_u_act, n - 1)
                layer_norm_scale(pool, n, s, NP)
            turns(pool, 0, turn)

            pool.wait_ge(s_route_in, 16 * 5)

            def turn(i, r):
                if live(i):
                    pool.wait_ge(s_mv, 2 * NP + i + 1)
                    layer_norm_scale(pool, i, r, 2 * NP)
                if live(i - 1):
                    n, s = i - 1, (r + 1) % 2
                    pair = [cut(t, s, T * D).rearrange("p (t d) -> p t d", t=T) for t in (y, y_gamma, y_beta)]
                    pool.wait_ge(s_yn, n + 1)
                    nc.gpsimd.tensor_tensor(pair[1], pair[0], gamma_sb[:].unsqueeze(1).to_broadcast([P, T, D]),
                                            ALU.mult).then_inc(s_yg, 1)
                    pool.wait_ge(s_yg, n + 1)
                    nc.gpsimd.tensor_tensor(pair[2], pair[1], beta_sb[:].unsqueeze(1).to_broadcast([P, T, D]),
                                            ALU.add).then_inc(s_yb, 1)
            turns(pool, 1, turn)

        @block.scalar
        def _(act):
            nc.scalar.preload_act_table_set("natural_log_exp_and_others")
            act.wait_ge(s_prep, PREP_ADJ)
            nc.scalar.activation(log_adj[:], rank[:], ACT.Ln).then_inc(s_prep_act, 1)

            def turn(i, r):
                if live(i - 2):
                    n, s = i - 2, r
                    act.wait_ge(s_z, n + 1)
                    nc.scalar.copy(cut(z_hi, s, T * D), cut(z, s, T * D)).then_inc(s_zhi, 1)
                if live(i - 3):
                    n, s = i - 3, (r + 1) % 2
                    act.wait_ge(s_G, n + 1)
                    nc.scalar.copy(cut(gathered, s, G * 2 * E), psum[:, 2 * s * 512:(2 * s + G) * 512]
                                   ).then_inc(s_gt, 1)
                if live(i - 4):
                    n, s = i - 4, r
                    act.wait_ge(s_vp, n + 1)
                    nc.scalar.mul(cut(q_low, s, G * E), banks[4 + s], SLOPE)
                    nc.scalar.copy(cut(v_sb, n, G * K * D), banks[6]).then_inc(s_vs, 1)
            turns(act, 4, turn)

            act.wait_ge(s_sm, SM_SHIFTED)
            nc.scalar.activation(expo[:], shifted[:], ACT.Exp).then_inc(s_sm_act, 1)

            def turn(i, r):
                if live(i - 2):
                    n, s = i - 2, r
                    act.wait_ge(s_y, n + 1)
                    nc.scalar.copy(cut(yT, s, G * N), banks[s]).then_inc(s_ys, 1)
                if live(i - 7):
                    n, s = i - 7, (r + 1) % 2
                    act.wait_ge(s_t, n + 1)
                    for g in range(G):
                        last = nc.scalar.activation(cut(uT_sb, n, G * N, g * N, N),
                                                    banks[4 + s][:, g * N:(g + 1) * N], ACT.Copy,
                                                    accum_out=cut(usum, n, G, g, 1))
                    last.then_inc(s_ut, 1)
                if live(i - 5):
                    n, s = i - 5, (r + 1) % 2
                    act.wait_ge(s_shift, n + 1)
                    if isinstance(i, int) and i >= NP:
                        act.wait_ge(s_t, n - 1)
                    for c in range(C):
                        t = C + c
                        last = nc.scalar.activation(cut(u, s * T + t, D), cut(x_sb, n, T * D, t * D, D),
                                                    ACT.Identity, bias=cut(shift, s, C, c, 1),
                                                    scale=cut(rstd, s, T, t, 1))
                    last.then_inc(s_u_act, 1)
            turns(act, 7, turn)

            act.wait_ge(s_rt, RT_SHIFT1)
            nc.scalar.activation(route[:, 3 * X:4 * X], route[:, 2 * X:3 * X], ACT.Exp).then_inc(s_rt_act, 1)
            act.wait_ge(s_rt, RT_SHIFT2)
            nc.scalar.activation(route[:, 9 * X:10 * X], route[:, 8 * X:9 * X], ACT.Exp).then_inc(s_rt_act, 1)
            act.wait_ge(s_rt, RT_DIFF)
            nc.scalar.activation(small[:, 8:9], small[:, 7:8], ACT.Exp).then_inc(s_rt_act, 1)
            nc.scalar.preload_act_table(ACT.Gelu)

            def choose_w1(n, s, g):
                for k in range(TOP):
                    off = nc.scalar.value_load(offsets_i[0:1, bass.ds((n * G + g) * TOP + k, 1)],
                                               min_val=0, max_val=(X - 1) * EW)
                    last = nc.scalar.copy(cut(w1_sel, (s * G + g) * TOP + k, F + FC),
                                          experts_sb[:, bass.ds(off, F + FC)])
                last.then_inc(s_w1, 1)

            act.wait_ge(s_experts, 16)
            act.wait_ge(s_rt, RT_OFFSETS)
            for g in range(G):
                choose_w1(0, 0, g)

            def turn(n, s):
                for g in range(G):
                    act.wait_ge(s_h, G * n + g + 1)
                    for k in range(TOP):
                        for c in range(FC):
                            m = (s * G + g) * TOP + k
                            last = nc.scalar.activation(
                                cut(hT, m * FC + c, N), banks[2 * g + k][:, c * N:(c + 1) * N], ACT.Gelu,
                                bias=cut(w1_sel, m, F + FC, F + c, 1))
                    last.then_inc(s_gelu, 1)
                    if live(n + 1) and not (isinstance(n, int) and n == NP - 1):
                        choose_w1(n + 1, (s + 1) % 2, g)
            for n in range(2):
                turn(n, n)
            with act.Fori(1, NP // 2 - 1) as j:
                turn(2 * j, 0)
                turn(2 * j + 1, 1)
            for n in range(NP - 2, NP):
                turn(n, n % 2)

        @block.vector
        def _(dve):
            prep = [0]

            def chain(ins, s, n, hold=True):
                n[0] += 1
                ins.then_inc(s, 1)
                if hold:
                    dve.wait_ge(s, n[0])

            dve.wait_ge(s_edges, 32)
            dve.wait_ge(s_const, 7)
            chain(nc.vector.tensor_copy(edges_col_f[:], edges_col_i[:]), s_prep, prep)
            chain(nc.vector.scalar_tensor_tensor(out=key_row[:], in0=edges_row_i[:], scalar=float(E),
                                                 in1=count_row[:], op0=ALU.mult, op1=ALU.add),
                  s_prep, prep, False)
            chain(nc.vector.scalar_tensor_tensor(out=key_col[:], in0=edges_col_f[:, 0:K], scalar=float(E),
                                                 in1=edge_col[:], op0=ALU.mult, op1=ALU.add), s_prep, prep)
            for k in range(K):
                chain(nc.vector.tensor_scalar(cut(before, k, E), key_row[:], key_col[:, k:k + 1], None,
                                              ALU.is_lt), s_prep, prep, k == K - 1)
            chain(nc.vector.tensor_reduce(rank[:], before[:].rearrange("p (k e) -> p k e", k=K),
                                          AX.X, ALU.add), s_prep, prep)
            for k in range(K):
                chain(nc.vector.tensor_scalar(cut(place, k, E), count_row[:], rank[:, k:k + 1], None,
                                              ALU.is_equal), s_prep, prep, False)
                for q in range(2):
                    chain(nc.vector.tensor_scalar(cut(placed, 2 * k + q, E), count_row[:], rank[:, k:k + 1],
                                                  edges_col_f[:, q * K + k:q * K + k + 1],
                                                  ALU.is_equal, ALU.mult), s_prep, prep, False)
            assert prep[0] == PREP_PLACED
            dve.wait_ge(s_prep_pe, 2)
            chain(nc.vector.tensor_copy(sorted_row[:], banks[0][:]), s_prep, prep, False)
            chain(nc.vector.tensor_copy(sorted_col[:], banks[1][:, 0:2 * K]), s_prep, prep)
            for c in range(C):
                for q, hot in enumerate((source_of, target_of)):
                    chain(nc.vector.tensor_scalar(cut(hot, c, E), cut(sorted_row, q, E),
                                                  node_col[:, c:c + 1], None, ALU.is_equal),
                          s_prep, prep, (c, q) == (C - 1, 1))
            for c in range(C):
                chain(nc.vector.tensor_tensor(cut(gather, 2 * c, E), cut(source_of, c, E),
                                              cut(target_of, c, E), ALU.add), s_prep, prep, False)
                chain(nc.vector.tensor_copy(cut(gather, 2 * c + 1, E), cut(target_of, c, E)),
                      s_prep, prep, False)
            assert prep[0] == PREP_GATHER
            nc.vector.memset(a_heads[:], 0.0).then_inc(s_prep, 1)
            prep[0] += 1
            dve.wait_ge(s_nets, 32)
            dve.wait_ge(s_prep, prep[0])
            for h in range(H):
                chain(nc.vector.tensor_copy(a_heads[h * DH:(h + 1) * DH, h:h + 1],
                                            a_sb[h * DH:(h + 1) * DH, :]), s_prep, prep, False)
            for k in range(K):
                chain(nc.vector.tensor_scalar(cut(spread, k, N), node_row[:],
                                              sorted_col[:, 2 * k:2 * k + 1], None, ALU.is_equal),
                      s_prep, prep, False)
                chain(nc.vector.tensor_scalar(cut(target_hot, k, N), count_row[:],
                                              sorted_col[:, 2 * k + 1:2 * k + 2], None, ALU.is_equal),
                      s_prep, prep, k == K - 1)
            dve.wait_ge(s_prep_pe, 3)
            chain(nc.vector.tensor_tensor(adj_pick[:], banks[2][:], target_hot[:], ALU.mult), s_prep, prep)
            chain(nc.vector.tensor_reduce(rank[:], adj_pick[:].rearrange("p (k m) -> p k m", k=K),
                                          AX.X, ALU.add), s_prep, prep)
            chain(nc.vector.tensor_scalar(rank[:], rank[:], LOG_EPS, None, ALU.add), s_prep, prep, False)
            assert prep[0] == PREP_ADJ
            chain(nc.vector.memset(same[:], 0.0), s_prep, prep)
            chain(nc.vector.tensor_tensor(same[:, 1:E], sorted_row[:, 1:E], sorted_row[:, 0:E - 1],
                                          ALU.is_equal), s_prep, prep)
            chain(nc.vector.tensor_scalar(start_low[:], same[:, 0:E], -LOW, LOW, ALU.mult, ALU.add),
                  s_prep, prep, False)
            chain(nc.vector.tensor_scalar(is_last[:], same[:, 1:E + 1], -1.0, 1.0, ALU.mult, ALU.add),
                  s_prep, prep)

            for n in range(XCH):
                dve.wait_ge(s_x[n], 16)

            def turn(i, r):
                if live(i - 1):
                    dve.wait_ge(s_stats, i)
                if live(i - 2):
                    n, s = i - 2, r
                    dve.wait_ge(s_rstd, n + 1)
                    normed(cut(z, s, T * D), cut(x_sb, n, T * D), s, range(T), s_z)
                if live(i - 1):
                    means((r + 1) % 2)
                if live(i):
                    statistics(cut(x_sb, i, T * D), r)
                if live(i - 2):
                    n, s = i - 2, r
                    dve.wait_ge(s_zhi, n + 1)
                    nc.vector.tensor_tensor(cut(z_lo, s, T * D), cut(z, s, T * D),
                                            cut(z_hi, s, T * D).bitcast(f32), ALU.subtract).then_inc(s_zlo, 1)
                if live(i - 4):
                    n, s = i - 4, r
                    dve.wait_ge(s_vs, n + 1)
                    nc.vector.tensor_tensor(cut(act_q, s, G * E), banks[4 + s], cut(q_low, s, G * E),
                                            ALU.max).then_inc(s_lr, 1)
            turns(dve, 4, turn)

            sm = [0]
            dve.wait_ge(s_e, NP)
            dve.wait_ge(s_prep_act, 1)
            for k in range(K):
                chain(nc.vector.tensor_scalar(
                    cut(logits_e, k, ROWS).rearrange("p (b h) -> p b h", h=H),
                    banks[7][:, 0:B * K * H].rearrange("p (b k h) -> p k b h", k=K, h=H)[:, k],
                    log_adj[:, k:k + 1], None, ALU.add), s_sm, sm, False)
            assert sm[0] == SM_LOGITS
            dve.wait_ge(s_sm_pe, 1)
            chain(nc.vector.tensor_copy(logits[:], banks[5][0:ROWS, 0:E]), s_sm, sm)
            chain(nc.vector.tensor_tensor_scan(scan[:], start_low[0:ROWS], logits[:], LOW, ALU.add, ALU.max),
                  s_sm, sm)
            chain(nc.vector.tensor_tensor(at_last[:], scan[:], is_last[0:ROWS], ALU.mult), s_sm, sm)
            chain(nc.vector.tensor_tensor_scan(seg_max[:, ::-1], same[0:ROWS, E:0:-1], at_last[:, ::-1], 0.0,
                                               ALU.mult, ALU.add), s_sm, sm)
            chain(nc.vector.tensor_tensor(shifted[:], logits[:], seg_max[:], ALU.subtract), s_sm, sm, False)
            assert sm[0] == SM_SHIFTED
            dve.wait_ge(s_sm_act, 1)
            chain(nc.vector.tensor_tensor_scan(scan[:], same[0:ROWS, 0:E], expo[:], 0.0, ALU.mult, ALU.add),
                  s_sm, sm)
            chain(nc.vector.tensor_tensor(at_last[:], scan[:], is_last[0:ROWS], ALU.mult), s_sm, sm)
            chain(nc.vector.tensor_tensor_scan(seg_sum[:, ::-1], same[0:ROWS, E:0:-1], at_last[:, ::-1], 0.0,
                                               ALU.mult, ALU.add), s_sm, sm)
            chain(nc.vector.reciprocal(scan[:], seg_sum[:]), s_sm, sm)
            chain(nc.vector.tensor_tensor(attn[:], expo[:], scan[:], ALU.mult), s_sm, sm, False)
            assert sm[0] == SM_ATTN
            dve.wait_ge(s_sm_pe, 2)
            chain(nc.vector.tensor_copy(attn_e[:].rearrange("p (b k h) -> p b k h", b=B, k=K),
                                        banks[5][:, 0:K * ROWS].rearrange("p (k b h) -> p b k h", k=K, b=B)),
                  s_sm, sm)

            def turn(i, r):
                if live(i - 3):
                    n, s = i - 3, (r + 1) % 2
                    pair = cut(x_sb, n, T * D)
                    dve.wait_ge(s_o, n + 1)
                    nc.vector.tensor_tensor(pair, banks[2 + s], pair, ALU.add).then_inc(s_x1, 1)
                if live(i):
                    if isinstance(i, int) and i == 2:
                        dve.wait_ge(s_y, 1)
                    weights = attn_e[:].rearrange("p (b k h) -> p (b k) h", b=B, k=K)
                    weights = weights[:, bass.ds(i * G * K, G * K)].unsqueeze(3)
                    nc.vector.tensor_tensor(
                        cut(av, r, G * K * D).rearrange("p (k h d) -> p k h d", k=G * K, h=H),
                        cut(v_sb, i, G * K * D).rearrange("p (k h d) -> p k h d", k=G * K, h=H),
                        weights.to_broadcast([P, G * K, H, DH]), ALU.mult).then_inc(s_av, 1)
                if live(i - 3):
                    dve.wait_ge(s_x1, i - 3 + 1)
                if live(i - 4):
                    dve.wait_ge(s_stats, NP + i - 4 + 1)
                if live(i - 5):
                    n, s = i - 5, (r + 1) % 2
                    dve.wait_ge(s_rstd, NP + n + 1)
                    if isinstance(i, int) and i >= NP:
                        dve.wait_ge(s_t, n - 1)
                    mean = cut(mean_var, s, 2 * T).rearrange("p (t k) -> p t k", k=2)[:, C:T, 0]
                    nc.vector.scalar_tensor_tensor(out=cut(shift, s, C), in0=mean, scalar=-1.0,
                                                   in1=cut(rstd, s, T, C, C), op0=ALU.mult,
                                                   op1=ALU.mult).then_inc(s_shift, 1)
                    normed(cut(u, s, T * D), cut(x_sb, n, T * D), s, range(C), s_u_dve)
                if live(i - 3):
                    statistics(cut(x_sb, i - 3, T * D), (r + 1) % 2)
                if live(i - 4):
                    means(r)
            turns(dve, 5, turn)

            rt = [0]

            def col(n):
                return route[:, n * X:(n + 1) * X]

            def softmax(at, out_at, src, n_act):
                chain(nc.vector.tensor_reduce(small[:, at:at + 1], src, AX.X, ALU.max), s_rt, rt)
                chain(nc.vector.tensor_scalar(col(out_at), src, small[:, at:at + 1], None, ALU.subtract),
                      s_rt, rt, False)
                dve.wait_ge(s_rt_act, n_act)
                chain(nc.vector.tensor_reduce(small[:, at + 1:at + 2], col(out_at + 1), AX.X, ALU.add), s_rt, rt)
                chain(nc.vector.reciprocal(small[:, at + 2:at + 3], small[:, at + 1:at + 2]), s_rt, rt)
                chain(nc.vector.tensor_scalar(col(out_at + 2), col(out_at + 1), small[:, at + 2:at + 3], None,
                                              ALU.mult), s_rt, rt)

            dve.wait_ge(s_route_in, 16 * 5)
            dve.wait_ge(s_rt_pe, 1)
            chain(nc.vector.scalar_tensor_tensor(out=col(1), in0=banks[6][0:B, 0:X], scalar=1.0 / N,
                                                 in1=br_sb[:], op0=ALU.mult, op1=ALU.add), s_rt, rt)
            softmax(0, 2, col(1), 1)
            assert rt[0] == RT_PROBS
            dve.wait_ge(s_rt_pe, 2)
            chain(nc.vector.tensor_scalar(col(5), banks[7][0:B, 0:X], float(N), None, ALU.mult), s_rt, rt)
            chain(nc.vector.reciprocal(col(6), col(5)), s_rt, rt)
            chain(nc.vector.tensor_scalar(col(6), col(6), CAPACITY, 1.0, ALU.mult, ALU.min), s_rt, rt)
            chain(nc.vector.tensor_tensor(col(7), col(4), col(6), ALU.mult), s_rt, rt)
            softmax(3, 8, col(7), 2)
            chain(nc.vector.max(col(11), col(10)), s_rt, rt)
            chain(nc.vector.max_index(top_i[:], col(11), col(10)), s_rt, rt)
            chain(nc.vector.tensor_tensor(small[:, 7:8], route[:, 11 * X + 1:11 * X + 2],
                                          route[:, 11 * X:11 * X + 1], ALU.subtract), s_rt, rt, False)
            assert rt[0] == RT_DIFF
            chain(nc.vector.tensor_copy(col(12), top_i[:]), s_rt, rt)
            dve.wait_ge(s_rt_act, 3)
            chain(nc.vector.tensor_scalar(small[:, 9:10], small[:, 8:9], 1.0, None, ALU.add), s_rt, rt)
            chain(nc.vector.reciprocal(small[:, 10:11], small[:, 9:10]), s_rt, rt)
            chain(nc.vector.tensor_tensor(small[:, 11:12], small[:, 10:11], small[:, 8:9], ALU.mult), s_rt, rt)
            chain(nc.vector.tensor_scalar(small[:, 12:12 + TOP], route[:, 12 * X:12 * X + TOP], float(EW), None,
                                          ALU.mult), s_rt, rt)
            chain(nc.vector.tensor_tensor(
                spread_w[:].rearrange("p (b q) -> p b q", q=2 * TOP),
                ident[0:B, 0:B].unsqueeze(2).to_broadcast([B, B, 2 * TOP]),
                small[:, 10:10 + 2 * TOP].unsqueeze(1).to_broadcast([B, B, 2 * TOP]), ALU.mult),
                s_rt, rt, False)
            for k in range(TOP):
                chain(nc.vector.tensor_scalar(col(13 + k), count_row[0:B, 0:X],
                                              route[:, 12 * X + k:12 * X + k + 1], small[:, 10 + k:11 + k],
                                              ALU.is_equal, ALU.mult), s_rt, rt, k == TOP - 1)
            chain(nc.vector.tensor_tensor(col(15), col(13), col(14), ALU.add), s_rt, rt, False)
            assert rt[0] == RT_DENSE
            dve.wait_ge(s_rt_pe, 4)
            chain(nc.vector.tensor_copy(dense_wT[:], banks[6][0:X, 0:B]), s_rt, rt, False)
            chain(nc.vector.tensor_copy(weight_bc[:], banks[7][:, 0:B * 2 * TOP]), s_rt, rt)
            assert rt[0] == RT_TURNED
            chain(nc.vector.tensor_copy(
                offsets_i[:].rearrange("p (b k) -> p b k", k=TOP),
                weight_bc[:].rearrange("p (b q) -> p b q", q=2 * TOP)[:, :, TOP:2 * TOP]), s_rt, rt)
            assert rt[0] == RT_OFFSETS
            dve.wait_ge(s_rt_pe, 5)
            chain(nc.vector.tensor_copy(b2_mix[:], banks[6][:, 0:B]), s_rt, rt)

            dve.wait_ge(s_experts, 16)

            def turn(i, r):
                if live(i - 3):
                    dve.wait_ge(s_tr, i - 3 + 1)
                if live(i - 2):
                    n, s = i - 2, r
                    dve.wait_ge(s_f, n + 1)
                    for g in range(G):
                        last = nc.vector.scalar_tensor_tensor(
                            out=cut(sT, s * G + g, N), in0=banks[4 + s][:, g * N:(g + 1) * N],
                            scalar=cut(b2_mix, n, G, g, 1), in1=cut(uT_sb, n, G * N, g * N, N),
                            op0=ALU.add, op1=ALU.add)
                    last.then_inc(s_s, 1)
                if live(i - 3):
                    statistics(banks[6 + (r + 1) % 2], (r + 1) % 2)
                    dve.wait_ge(s_stats, 2 * NP + i - 3 + 1)
                if live(i - 5):
                    n, s = i - 5, (r + 1) % 2
                    pair = cut(x_sb, n, T * D)
                    dve.wait_ge(s_yb, n + 1)
                    nc.vector.tensor_tensor(pair, cut(y_beta, s, T * D), pair, ALU.add).then_inc(s_res, 1)
                if live(i - 3):
                    means((r + 1) % 2)
                if live(i):
                    for m in range(G * TOP):
                        off = nc.vector.value_load(offsets_i[0:1, bass.ds(i * G * TOP + m, 1)],
                                                   min_val=0, max_val=(X - 1) * EW)
                        g, k = m // TOP, m % TOP
                        last = nc.vector.tensor_scalar(
                            cut(w2_sel, r * G * TOP + m, FC * D), experts_sb[:, bass.ds(off + F + FC, FC * D)],
                            cut(weight_bc, i, G * 2 * TOP, g * 2 * TOP + k, 1), None, ALU.mult)
                    last.then_inc(s_w2, 1)
                if live(i - 3):
                    n, s = i - 3, (r + 1) % 2
                    dve.wait_ge(s_rstd, 2 * NP + n + 1)
                    normed(cut(y, s, T * D), banks[6 + s], s, range(T), s_yn)
            turns(dve, 5, turn)

        @block.tensor
        def _(pe):
            def mm(out_, lhsT, rhs, start=True, stop=True):
                return nc.tensor.matmul(out_, lhsT, rhs, start=start, stop=stop)

            pe.wait_ge(s_prep, PREP_PLACED)
            pe.wait_ge(s_const, 7)
            for k in range(K):
                last = mm(banks[0][:], ones[:], cut(placed, k, 2 * E), k == 0, k == K - 1)
            last.then_inc(s_prep_pe, 1)
            for j in range(K):
                for k in range(K):
                    last = mm(banks[1][:, 2 * j:2 * j + 2], cut(place, k, E, j * P, P),
                              edges_col_f[:].rearrange("p (q k) -> p k q", k=K)[:, k], k == 0, k == K - 1)
            last.then_inc(s_prep_pe, 1)
            pe.wait_ge(s_prep, PREP_GATHER)
            pe.wait_ge(s_adj, 16)
            for k in range(K):
                for c in range(C):
                    last = mm(banks[2][:, k * N:(k + 1) * N], cut(source_of, c, E, k * P, P),
                              cut(adj_sb, c, N), c == 0, c == C - 1)
            last.then_inc(s_prep_pe, 1)
            pe.wait_ge(s_prep, PREP_ADJ)

            def turn(i, r):
                if live(i - 2):
                    n, s = i - 2, r
                    pe.wait_ge(s_zlo, n + 1)
                    for g in range(G):
                        for c in range(C):
                            for part in (z_hi, z_lo):
                                last = mm(banks[2 * s + g], cut(part, s * T + g * C + c, D),
                                          cut(gather, c, 2 * E),
                                          c == 0 and part is z_hi, c == C - 1 and part is z_lo)
                    last.then_inc(s_G, 1)
                if live(i - 3):
                    n, s = i - 3, (r + 1) % 2
                    pe.wait_ge(s_gt, n + 1)
                    for g in range(G):
                        mm(banks[4 + s][:, g * E:(g + 1) * E], W_LIN, cut(gathered, s * G + g, 2 * E, 0, E))
                    if not isinstance(n, int) or n >= 1:
                        pe.wait_ge(s_vs, n)
                    for g in range(G):
                        for k in range(K):
                            last = mm(banks[6][:, (g * K + k) * D:(g * K + k + 1) * D],
                                      cut(gathered, s * G + g, 2 * E, E + k * P, P), W_VAL)
                    last.then_inc(s_vp, 1)
                if live(i - 4):
                    n, s = i - 4, r
                    pe.wait_ge(s_lr, n + 1)
                    for m in range(G * K):
                        last = mm(cut(banks[7], n, G * K * H, m * H, H), cut(act_q, s * G * K + m, P), a_heads[:])
                    last.then_inc(s_e, 1)
            turns(pe, 4, turn)

            pe.wait_ge(s_ident, 2)
            pe.wait_ge(s_sm, SM_LOGITS)
            for k in range(K):
                last = nc.tensor.transpose(banks[5][0:ROWS, k * P:(k + 1) * P], cut(logits_e, k, ROWS), ident[:])
            last.then_inc(s_sm_pe, 1)
            pe.wait_ge(s_sm, SM_ATTN)
            for k in range(K):
                last = nc.tensor.transpose(banks[5][:, k * ROWS:(k + 1) * ROWS], attn[:, k * P:(k + 1) * P],
                                           ident[0:ROWS, 0:ROWS])
            last.then_inc(s_sm_pe, 1)

            def turn(i, r):
                if live(i - 6):
                    n, s = i - 6, r
                    pe.wait_ge(s_u_dve, n + 1)
                    pe.wait_ge(s_u_act, n + 1)
                    for t in range(T):
                        last = nc.tensor.transpose(banks[4 + s][:, t * P:(t + 1) * P],
                                                   cut(u, s * T + t, D), ident[:])
                    last.then_inc(s_t, 1)
                if live(i - 1):
                    n, s = i - 1, (r + 1) % 2
                    pe.wait_ge(s_av, n + 1)
                    for g in range(G):
                        for k in range(K):
                            last = mm(banks[s][:, g * N:(g + 1) * N], cut(av, (s * G + g) * K + k, D),
                                      cut(spread, k, N), k == 0, k == K - 1)
                    last.then_inc(s_y, 1)
                if live(i - 2):
                    n, s = i - 2, r
                    pe.wait_ge(s_ys, n + 1)
                    if isinstance(n, int) and n == NP - 1:
                        pe.wait_ge(s_x1, n - 1)
                    for t in range(T):
                        last = mm(banks[2 + s][:, t * D:(t + 1) * D], cut(yT, s * T + t, P), W_OUT)
                    last.then_inc(s_o, 1)
            turns(pe, 6, turn)

            pe.wait_ge(s_route_in, 16 * 5)
            pe.wait_ge(s_ut, NP)
            mm(banks[6][0:B, 0:X], usum[:], router_sb[:]).then_inc(s_rt_pe, 1)
            pe.wait_ge(s_rt, RT_PROBS)
            mm(banks[7][0:B, 0:X], ones[0:B, 0:B], route[:, 4 * X:5 * X]).then_inc(s_rt_pe, 1)
            pe.wait_ge(s_rt, RT_DENSE)
            nc.tensor.transpose(banks[6][0:X, 0:B], route[:, 15 * X:16 * X], ident[0:B, 0:B]).then_inc(s_rt_pe, 1)
            mm(banks[7][:, 0:B * 2 * TOP], ones[0:B, :], spread_w[:]).then_inc(s_rt_pe, 1)
            pe.wait_ge(s_rt, RT_TURNED)
            mm(banks[6][:, 0:B], b2_sb[:], dense_wT[:]).then_inc(s_rt_pe, 1)
            pe.wait_ge(s_rt, RT_OFFSETS + 1)

            def turn(i, r):
                for g in range(G):
                    if live(i):
                        n, s = i, r
                        pe.wait_ge(s_w1, G * n + g + 1)
                        if not isinstance(n, int) or n >= 1:
                            pe.wait_ge(s_gelu, G * (n - 1) + g + 1)
                        for k in range(TOP):
                            for c in range(FC):
                                last = mm(banks[2 * g + k][:, c * N:(c + 1) * N],
                                          cut(w1_sel, (s * G + g) * TOP + k, F + FC, c * P, P),
                                          cut(uT_sb, n, G * N, g * N, N))
                        last.then_inc(s_h, 1)
                    if live(i - 2) and g == 0:
                        n, s = i - 2, r
                        pe.wait_ge(s_s, n + 1)
                        for t in range(T):
                            last = nc.tensor.transpose(banks[6 + s][:, t * P:(t + 1) * P],
                                                       cut(sT, s * T + t, P), ident[:])
                        last.then_inc(s_tr, 1)
                    if live(i - 1):
                        n, s = i - 1, (r + 1) % 2
                        if g == 0:
                            pe.wait_ge(s_w2, n + 1)
                        pe.wait_ge(s_gelu, G * n + g + 1)
                        for k in range(TOP):
                            for c in range(FC):
                                m = (s * G + g) * TOP + k
                                last = mm(banks[4 + s][:, g * N:(g + 1) * N], cut(w2_sel, m * FC + c, D),
                                          cut(hT, m * FC + c, N), k == 0 and c == 0,
                                          k == TOP - 1 and c == FC - 1)
                        if g == G - 1:
                            last.then_inc(s_f, 1)
            turns(pe, 2, turn)


PREP_PLACED = 12
PREP_GATHER = 22
PREP_ADJ = 34
SM_LOGITS = 2
SM_SHIFTED = 7
SM_ATTN = 12
RT_SHIFT1 = 3
RT_PROBS = 6
RT_SHIFT2 = 12
RT_DIFF = 18
RT_DENSE = 27
RT_TURNED = 29
RT_OFFSETS = 30


def kernel(**inputs):
    import numpy as np
    import concourse.bacc as bacc
    from concourse import mybir
    from concourse.bass_utils import run_bass_kernel_spmd

    get = {k: np.asarray(v) for k, v in inputs.items()}
    P = 128
    W1, b1, W2 = get["L0_ffn_W1"], get["L0_ffn_b1"], get["L0_ffn_W2"]
    X, D, F = W1.shape
    src, dst = get["L0_gnn_src"], get["L0_gnn_dst"]
    K = src.shape[0] // P
    arrays = {
        "x": get["x"],
        "adj": get["adj"],
        "nets": np.concatenate([get["L0_gnn_W_lin"].T, get["L0_gnn_W_val"].T, get["L0_gnn_W_out"].T], axis=1),
        "a_col": get["L0_gnn_a"].reshape(D, 1),
        "router": get["L0_ffn_Wr"],
        "experts": np.concatenate([W1.transpose(1, 0, 2), b1.reshape(X, F // P, P).transpose(2, 0, 1),
                                   W2.reshape(X, F // P, P, D).transpose(2, 0, 1, 3).reshape(P, X, -1)],
                                  axis=2).reshape(P, -1),
        "edges_row": src.reshape(1, -1),
        "edges_col": np.concatenate([src.reshape(K, P).T, dst.reshape(K, P).T], axis=1),
        "br": get["L0_ffn_br"],
        "b2": get["L0_ffn_b2"],
        "gamma": get["L0_ffn_gamma"],
        "beta": get["L0_ffn_beta"],
    }
    nc = bacc.Bacc("TRN2", target_bir_lowering=False, num_devices=1)
    given, args = {}, []
    for name, a in arrays.items():
        a = np.ascontiguousarray(a)
        given[f"in_{name}"] = a
        args.append(nc.dram_tensor(f"in_{name}", a.shape, mybir.dt.from_np(a.dtype), kind="ExternalInput").ap())
    args.append(nc.dram_tensor("out_y", get["x"].shape, mybir.dt.float32, kind="ExternalOutput").ap())
    gnn_moe_program(nc, *args)
    r = run_bass_kernel_spmd(nc, [given], core_ids=[0])
    return r.results[0]["out_y"]
```

```python
import concourse.bass as bass
from concourse import mybir
from contextlib import ExitStack


def gnn_moe_program(nc, x, adj, nets, a_row, router, w1, w2, edges_row, edges_col, br, biases, gamma, beta, out):
    f32 = mybir.dt.float32
    f32r = mybir.dt.float32r
    i32 = mybir.dt.int32
    u32 = mybir.dt.uint32
    ALU = mybir.AluOpType
    ACT = mybir.ActivationFunctionType
    AX = mybir.AxisListType
    ACTIVATION, VECTOR = mybir.EngineType.Activation, mybir.EngineType.DVE

    P = 128
    B, N, D = x.shape
    C = N // P
    E = edges_row.shape[1]
    K = E // P
    H = 4
    DH = D // H
    X = br.shape[0]
    F = w1.shape[1] // X
    FC = F // P
    EW = F
    assert EW == FC * D
    TOP = 2
    ROWS = B * H
    G = 2
    NP = B // G
    T = G * C
    CAPACITY = float(-(-B * N * 5 // 4 // X))
    SLOPE = 0.2
    LN_EPS = 1e-5
    LOG_EPS = 1e-8
    LOW = -1e30

    ctx = ExitStack()
    with ctx:
        def sb(name, shape, dt=f32):
            return ctx.enter_context(nc.sbuf_tensor(name, shape, dt))

        def sem(name):
            return ctx.enter_context(nc.semaphore(name))

        x_sb = sb("x_sb", [P, B * N // P * D])
        v_sb = sb("v_sb", [P, B * K * D])
        uT_sb = v_sb
        nets_sb = sb("nets_sb", [P, 3 * D])
        w1_parts = sb("w1_parts", [P, 2 * X * EW], f32r)
        w2_sb = sb("w2_sb", [P, X * EW])
        gamma_sb = sb("gamma_sb", [P, D])
        beta_sb = sb("beta_sb", [P, D])
        router_sb = sb("router_sb", [P, X])
        br_sb = sb("br_sb", [B, X])
        biases_sb = sb("biases_sb", [X, F + D])
        adj_sb = sb("adj_sb", [P, C * N])
        a_sb = sb("a_sb", [P, D])
        ident = sb("ident", [P, P])
        ones = sb("ones", [P, P])
        minus_half = sb("minus_half", [P, T])
        minus_one = sb("minus_one", [P, T])
        ln_eps = sb("ln_eps", [P, T])
        log_eps = sb("log_eps", [P, 1])
        usum = sb("usum", [P, B])

        edges_row_i = sb("edges_row_i", [P, E], i32)
        edges_col_i = sb("edges_col_i", [P, 2 * K], i32)
        edges_col_f = sb("edges_col_f", [P, 2 * K])
        count_row = sb("count_row", [P, N])
        node_row = sb("node_row", [P, N])
        node_col = sb("node_col", [P, C])
        edge_col = sb("edge_col", [P, K])
        key_row = sb("key_row", [P, E])
        key_col = sb("key_col", [P, K])
        before = sb("before", [P, K * E])
        rank = sb("rank", [P, K])
        place = sb("place", [P, K * E], f32r)
        edges_col_r = sb("edges_col_r", [P, 2 * K], f32r)
        placed = sb("placed", [P, K * 2 * E], f32r)
        ones_r = sb("ones_r", [P, P], f32r)
        sorted_row = sb("sorted_row", [P, 2 * E])
        sorted_col = sb("sorted_col", [P, K * 2])
        gather = sb("gather", [P, C * 2 * E], f32r)
        source_of = sb("source_of", [P, C * E])
        spread = sb("spread", [P, K * N])
        adj_edge = sb("adj_edge", [P, K])
        log_adj = sb("log_adj", [P, K])
        same = sb("same", [P, E + 1])
        start_low = sb("start_low", [P, E])
        is_last = sb("is_last", [P, E])

        stats = sb("stats", [P, 2 * T * 6])
        mean_var = sb("mean_var", [P, 2 * T * 2])
        var_eps = sb("var_eps", [P, 2 * T])
        rstd = sb("rstd", [P, 2 * T])
        minus_mean = sb("minus_mean", [P, 2 * T])
        shift = sb("shift", [P, 2 * T])
        z = sb("z", [P, 2 * T * D])
        z_hi = sb("z_hi", [P, 2 * T * D], f32r)
        z_lo = sb("z_lo", [P, 2 * T * D], f32r)
        gathered = sb("gathered", [P, 2 * G * 2 * E])
        q_low = sb("q_low", [P, 2 * G * E])
        act_q = sb("act_q", [P, 2 * G * E])
        av = sb("av", [P, 2 * G * K * D])
        target_hot, adj_pick = av[:, 0:K * N], av[:, K * N:2 * K * N]
        yT = sb("yT", [P, 2 * G * N])
        u = sb("u", [P, 2 * T * D])

        weighed = u
        logits_e = sb("logits_e", [P, K * ROWS])
        scan = sb("scan", [ROWS, E])
        at_last = sb("at_last", [ROWS, E])
        seg_max = sb("seg_max", [ROWS, E])
        shifted = sb("shifted", [ROWS, E])
        expo = sb("expo", [ROWS, E])
        seg_sum = sb("seg_sum", [ROWS, E])
        attn = sb("attn", [ROWS, E])
        raw_logits = attn
        attn_e = sb("attn_e", [P, K * ROWS])

        route = sb("route", [B, 17 * X])
        top_i = sb("top_i", [B, 8], u32)
        small = sb("small", [B, 14])
        spread_w = sb("spread_w", [B, B * 2 * TOP])
        expertT = sb("expertT", [X, (TOP + 1) * B])
        weight_bc = sb("weight_bc", [P, B * 2 * TOP])
        offsets_i = sb("offsets_i", [P, B * TOP], i32)
        b1_sel = sb("b1_sel", [P, FC * TOP * B])
        b2_mix = sb("b2_mix", [P, B])

        w1_sel = sb("w1_sel", [P, 2 * G * TOP * 2 * EW], f32r)
        w2_sel = gathered
        hT = sb("hT", [P, 2 * G * TOP * FC * N])
        sT = yT
        w1_sb = hT
        uT_hi, uT_lo = z_hi, z_lo
        centred = q_low

        psum = ctx.enter_context(nc.psum_tensor("psum", [P, 8 * 512], f32))
        banks = [psum[:, n * 512:(n + 1) * 512] for n in range(8)]

        XCH = 8
        x_in = [sem(f"x_in{n}") for n in range(XCH)]
        edges_in, nets_in, adj_in, params_in, w1_in = (
            sem(n) for n in ("edges_in", "nets_in", "adj_in", "params_in", "w1_in"))
        w2_in = sem("w2_in")
        constants_set, ident_set, prep_steps, sorted_ready, sorted_copied = (
            sem(n) for n in ("constants_set", "ident_set", "prep_steps", "sorted_ready", "sorted_copied"))
        hots_ready, same_ready, adj_rows_ready, adj_picked, log_adj_ready = (
            sem(n) for n in ("hots_ready", "same_ready", "adj_rows_ready", "adj_picked", "log_adj_ready"))
        stats_ready, means_ready, var_eps_ready, scale_ready = (
            sem(n) for n in ("stats_ready", "means_ready", "var_eps_ready", "scale_ready"))
        shift1_ready, z_dve_ready, z_act_ready, z_hi_ready, z_lo_ready = (
            sem(n) for n in ("shift1_ready", "z_dve_ready", "z_act_ready", "z_hi_ready", "z_lo_ready"))
        gather_ready, gathered_copied, q_ready, v_ready, q_low_ready = (
            sem(n) for n in ("gather_ready", "gathered_copied", "q_ready", "v_ready", "q_low_ready"))
        v_copied, leaky_ready, weighed_ready, last_weighed_ready, logits_ready = (
            sem(n) for n in ("v_copied", "leaky_ready", "weighed_ready", "last_weighed_ready", "logits_ready"))
        softmax_steps, softmax_turned, exp_ready, w1_hi_ready, w1_lo_ready = (
            sem(n) for n in ("softmax_steps", "softmax_turned", "exp_ready", "w1_hi_ready", "w1_lo_ready"))
        av_ready, y_ready, y_copied, gnn_ready, x1_ready = (
            sem(n) for n in ("av_ready", "y_ready", "y_copied", "gnn_ready", "x1_ready"))
        shift2_ready, u_dve_ready, u_act_ready, u_turned, uT_ready = (
            sem(n) for n in ("shift2_ready", "u_dve_ready", "u_act_ready", "u_turned", "uT_ready"))
        routing_steps, routing_products, routing_exps = (
            sem(n) for n in ("routing_steps", "routing_products", "routing_exps"))
        uT_hi_ready, uT_lo_ready, x_beta_ready, w1_chosen, w2_chosen = (
            sem(n) for n in ("uT_hi_ready", "uT_lo_ready", "x_beta_ready", "w1_chosen", "w2_chosen"))
        hidden_ready, gelu_ready, ffn_ready, sum_ready, sum_turned = (
            sem(n) for n in ("hidden_ready", "gelu_ready", "ffn_ready", "sum_ready", "sum_turned"))
        centred_ready, result_ready, result_stored = (
            sem(n) for n in ("centred_ready", "result_ready", "result_stored"))

        block = ctx.enter_context(nc.Block())

        def live(n):
            return not isinstance(n, int) or 0 <= n < NP

        def turns(eng, lag, turn, first=0):
            head = max(lag + lag % 2, 2)
            for i in range(first, head):
                turn(i, i % 2)
            with eng.Fori(head // 2, NP // 2) as j:
                turn(2 * j, 0)
                turn(2 * j + 1, 1)
            for i in range(NP, NP + lag):
                turn(i, i % 2)

        def cut(t, b, width, at=0, n=None):
            return t[:, bass.ds(b * width + at, width if n is None else n)]

        def load_offsets(engine, first, graphs=G):
            _, values = nc.values_load_multi_w_load_instructions(
                offsets_i[0:1, bass.ds(first * TOP, graphs * TOP)], engines=[engine], min_val=0, max_val=(X - 1) * EW,
                skip_runtime_bounds_check_because="the offsets are clamped to the table where they are computed")
            return values

        W_LIN, W_VAL, W_OUT = (nets_sb[:, n * D:(n + 1) * D] for n in range(3))

        def layer_norm_scale(pool, n, s, done):
            var = cut(mean_var, s, 2 * T).rearrange("p (t k) -> p t k", k=2)[:, :, 1]
            nc.gpsimd.tensor_tensor(cut(var_eps, s, T), var, ln_eps[:, :], ALU.add).then_inc(var_eps_ready, 1)
            pool.wait_ge(var_eps_ready, done + n + 1)
            nc.gpsimd.tensor_tensor(cut(rstd, s, T), cut(var_eps, s, T), minus_half[:, :],
                                    ALU.pow).then_inc(scale_ready, 1)

        def layer_norm_shift(pool, n, s, done, shift_done):
            mean = cut(mean_var, s, 2 * T).rearrange("p (t k) -> p t k", k=2)[:, :, 0]
            nc.gpsimd.tensor_tensor(cut(minus_mean, s, T), mean, minus_one[:, :], ALU.mult)
            layer_norm_scale(pool, n, s, done)
            pool.wait_ge(scale_ready, done + n + 1)
            nc.gpsimd.tensor_tensor(cut(shift, s, T), cut(minus_mean, s, T), cut(rstd, s, T),
                                    ALU.mult).then_inc(shift_done, 1)

        def times_a(engine, n, s, done):
            engine.tensor_tensor(
                cut(weighed, s, G * K * D).rearrange("p (m d) -> p m d", d=D),
                cut(act_q, s, G * K * D).rearrange("p (m d) -> p m d", d=D),
                a_sb[:].unsqueeze(1).to_broadcast([P, G * K, D]), ALU.mult).then_inc(done, 1)

        def statistics(src, s):
            for t in range(T):
                last = nc.vector.bn_stats(cut(stats, s, T * 6, t * 6, 6), src[:, t * D:(t + 1) * D])
            last.then_inc(stats_ready, 1)

        def means(s):
            for t in range(T):
                last = nc.vector.bn_aggr(cut(mean_var, s, T * 2, t * 2, 2), cut(stats, s, T * 6, t * 6, 6))
            last.then_inc(means_ready, 1)

        def normed(dst, src, s, slots, done):
            for t in slots:
                last = nc.vector.tensor_scalar(dst[:, t * D:(t + 1) * D], src[:, t * D:(t + 1) * D],
                                               cut(mean_var, s, 2 * T, 2 * t, 1), cut(rstd, s, T, t, 1),
                                               ALU.subtract, ALU.mult)
            last.then_inc(done, 1)

        @block.sync
        def _(sp):
            step = B // XCH

            def load_x(n):
                sp.dma_start(x_sb[:, n * step * C * D:(n + 1) * step * C * D]
                             .rearrange("p (b k) -> p b k", b=step),
                             x[n * step:(n + 1) * step].rearrange("b (p c) d -> p b (c d)", p=P)
                             ).then_inc(x_in[n], 16)

            sp.dma_start(edges_row_i[:], edges_row[0].partition_broadcast(P)).then_inc(edges_in, 16)
            sp.dma_start(edges_col_i[:], edges_col).then_inc(edges_in, 16)
            load_x(0)
            sp.dma_start(nets_sb[:], nets).then_inc(nets_in, 16)
            sp.dma_start(a_sb[:], a_row.partition_broadcast(P)).then_inc(nets_in, 16)
            sp.dma_start(adj_sb[:].rearrange("p (c m) -> p c m", c=C),
                         adj.rearrange("(p c) m -> p c m", p=P)).then_inc(adj_in, 16)
            for n in range(1, XCH):
                load_x(n)
            sp.dma_start(router_sb[:], router).then_inc(params_in, 16)
            sp.dma_start(br_sb[:], br.partition_broadcast(B)).then_inc(params_in, 16)
            sp.dma_start(biases_sb[:], biases).then_inc(params_in, 16)
            sp.dma_start(gamma_sb[:], gamma.partition_broadcast(P)).then_inc(params_in, 16)
            sp.dma_start(beta_sb[:], beta.partition_broadcast(P)).then_inc(params_in, 16)
            sp.dma_start(w1_sb[:, 0:X * EW], w1).then_inc(w1_in, 16)
            sp.dma_start(w2_sb[:], w2).then_inc(w2_in, 16)
            with sp.Fori(0, NP) as n:
                sp.wait_ge(result_ready, n + 1)
                sp.dma_start(out[bass.ds(n * G, G)].rearrange("b (p c) d -> p b (c d)", p=P),
                             cut(x_sb, n, T * D).rearrange("p (b k) -> p b k", b=G)).then_inc(result_stored, 16)
            sp.wait_ge(result_stored, 16 * NP)

        @block.gpsimd
        def _(pool):
            nc.gpsimd.iota(count_row[:], [[1, N]], base=0, channel_multiplier=0,
                           allow_small_or_imprecise_dtypes=True).then_inc(constants_set, 1)
            nc.gpsimd.iota(edge_col[:], [[P, K]], base=0, channel_multiplier=1,
                           allow_small_or_imprecise_dtypes=True).then_inc(constants_set, 1)
            nc.gpsimd.iota(node_col[:], [[1, C]], base=0, channel_multiplier=C,
                           allow_small_or_imprecise_dtypes=True).then_inc(constants_set, 1)
            nc.gpsimd.iota(node_row[:].rearrange("p (c n) -> p c n", c=C), [[1, C], [C, P]], base=0,
                           channel_multiplier=0, allow_small_or_imprecise_dtypes=True).then_inc(constants_set, 1)
            nc.gpsimd.memset(log_eps[:], LOG_EPS).then_inc(constants_set, 1)
            nc.gpsimd.memset(same[:], 0.0).then_inc(constants_set, 1)
            nc.gpsimd.memset(ones[:], 1.0).then_inc(constants_set, 1)
            nc.gpsimd.memset(minus_half[:], -0.5).then_inc(constants_set, 1)
            nc.gpsimd.memset(minus_one[:], -1.0).then_inc(constants_set, 1)
            nc.gpsimd.memset(ln_eps[:], LN_EPS).then_inc(constants_set, 1)
            nc.gpsimd.memset(ident[:], 0.0).then_inc(ident_set, 1)
            pool.wait_ge(ident_set, 1)
            nc.gpsimd.affine_select(out=ident[:], in_=ident[:], compare_op=ALU.not_equal, fill=1.0, base=0,
                                    pattern=[[-1, P]], channel_multiplier=1).then_inc(ident_set, 1)
            pool.wait_ge(constants_set, CONSTANTS)

            pool.wait_ge(nets_in, 32)

            def turn(i, r):
                if live(i - 1):
                    n, s = i - 1, (r + 1) % 2
                    pool.wait_ge(means_ready, n + 1)
                    layer_norm_shift(pool, n, s, 0, shift1_ready)
                if live(i - 5) and not (isinstance(i, int) and i - 5 == NP - 1):
                    n, s = i - 5, (r + 1) % 2
                    pool.wait_ge(leaky_ready, n + 1)
                    times_a(nc.gpsimd, n, s, weighed_ready)
            turn(0, 0)
            turn(1, 1)
            turn(2, 0)
            pool.wait_ge(sorted_copied, 2)
            for k in range(K):
                nc.gpsimd.tensor_scalar(cut(target_hot, k, N), count_row[:], sorted_col[:, 2 * k + 1:2 * k + 2],
                                        None, ALU.is_equal).then_inc(hots_ready, 1)
            turn(3, 1)
            turns(pool, 5, turn, 4)

            pool.wait_ge(same_ready, 1)
            nc.gpsimd.tensor_scalar(start_low[:], same[:, 0:E], -LOW, LOW, ALU.mult, ALU.add).then_inc(hots_ready, 1)
            nc.gpsimd.tensor_scalar(is_last[:], same[:, 1:E + 1], -1.0, 1.0, ALU.mult,
                                    ALU.add).then_inc(hots_ready, 1)

            for k in range(K):
                nc.gpsimd.tensor_scalar(cut(spread, k, N), node_row[:], sorted_col[:, 2 * k:2 * k + 1], None,
                                        ALU.is_equal).then_inc(hots_ready, 1)

            pool.wait_ge(w1_hi_ready, 1)
            nc.gpsimd.tensor_tensor(w1_parts[:, X * EW:2 * X * EW], w1_sb[:, 0:X * EW],
                                    w1_parts[:, 0:X * EW].bitcast(f32), ALU.subtract).then_inc(w1_lo_ready, 1)

            def turn(n, s):
                pool.wait_ge(means_ready, NP + n + 1)
                if not isinstance(n, int) or n >= 2:
                    pool.wait_ge(u_act_ready, n - 1)
                    pool.wait_ge(u_dve_ready, n - 1)
                layer_norm_shift(pool, n, s, NP, shift2_ready)
            turns(pool, 0, turn)

            pool.wait_ge(params_in, PARAMS)

            def turn(i, r):
                if live(i):
                    pool.wait_ge(uT_hi_ready, i + 1)
                    nc.gpsimd.tensor_tensor(cut(uT_lo, r, G * N), cut(uT_sb, i, G * N),
                                            cut(uT_hi, r, G * N).bitcast(f32), ALU.subtract).then_inc(uT_lo_ready, 1)
                if live(i - 3):
                    pool.wait_ge(means_ready, 2 * NP + i - 3 + 1)
                    layer_norm_scale(pool, i - 3, (r + 1) % 2, 2 * NP)
                if live(i):
                    pair = cut(x_sb, i, T * D).rearrange("p (t d) -> p t d", t=T)
                    nc.gpsimd.tensor_tensor(pair, pair, beta_sb[:].unsqueeze(1).to_broadcast([P, T, D]),
                                            ALU.add).then_inc(x_beta_ready, 1)
            turns(pool, 3, turn)

        @block.scalar
        def _(act):
            nc.scalar.preload_act_table_set("natural_log_exp_and_others")
            act.wait_ge(sorted_ready, 2)
            act.wait_ge(prep_steps, PREP_GATHER)
            nc.scalar.copy(sorted_row[:], banks[6]).then_inc(sorted_copied, 1)
            nc.scalar.copy(sorted_col[:], banks[7][:, 0:2 * K]).then_inc(sorted_copied, 1)

            def turn(i, r):
                if live(i - 2):
                    n, s = i - 2, r
                    act.wait_ge(shift1_ready, n + 1)
                    for t in range(C, T):
                        last = nc.scalar.activation(cut(z, s * T + t, D), cut(x_sb, n, T * D, t * D, D),
                                                    ACT.Identity, bias=cut(shift, s, T, t, 1),
                                                    scale=cut(rstd, s, T, t, 1))
                    last.then_inc(z_act_ready, 1)
                    act.wait_ge(z_act_ready, n + 1)
                    act.wait_ge(z_dve_ready, n + 1)
                    nc.scalar.copy(cut(z_hi, s, T * D), cut(z, s, T * D)).then_inc(z_hi_ready, 1)
                if live(i - 3):
                    n, s = i - 3, (r + 1) % 2
                    act.wait_ge(gather_ready, n + 1)
                    nc.scalar.copy(cut(gathered, s, G * 2 * E), psum[:, 2 * s * 512:(2 * s + G) * 512]
                                   ).then_inc(gathered_copied, 1)
                if live(i - 4):
                    n, s = i - 4, r
                    act.wait_ge(q_ready, n + 1)
                    nc.scalar.mul(cut(q_low, s, G * E), banks[4 + s], SLOPE).then_inc(q_low_ready, 1)
                    act.wait_ge(v_ready, n + 1)
                    nc.scalar.copy(cut(v_sb, n, G * K * D), banks[6 + s]).then_inc(v_copied, 1)
            turns(act, 4, turn)

            act.wait_ge(adj_picked, 2)
            nc.scalar.activation(log_adj[:], adj_edge[:], ACT.Ln, bias=log_eps[:]).then_inc(log_adj_ready, 1)
            act.wait_ge(softmax_steps, SM_SHIFTED)
            nc.scalar.activation(expo[:], shifted[:], ACT.Exp).then_inc(exp_ready, 1)
            act.wait_ge(w1_in, 16)
            nc.scalar.copy(w1_parts[:, 0:X * EW], w1_sb[:, 0:X * EW]).then_inc(w1_hi_ready, 1)

            def turn(i, r):
                if live(i - 2):
                    n, s = i - 2, r
                    act.wait_ge(y_ready, n + 1)
                    nc.scalar.copy(cut(yT, s, G * N), banks[s]).then_inc(y_copied, 1)
                if live(i - 8):
                    n, s = i - 8, r
                    act.wait_ge(u_turned, n + 1)
                    for g in range(G):
                        last = nc.scalar.activation(cut(uT_sb, n, G * N, g * N, N),
                                                    banks[4 + s][:, g * N:(g + 1) * N], ACT.Copy,
                                                    accum_out=cut(usum, n, G, g, 1))
                    last.then_inc(uT_ready, 1)
                if live(i - 6):
                    n, s = i - 6, r
                    act.wait_ge(shift2_ready, n + 1)
                    if isinstance(i, int) and i >= NP:
                        act.wait_ge(u_turned, n - 1)
                    for c in range(C):
                        t = C + c
                        last = nc.scalar.activation(cut(u, s * T + t, D), cut(x_sb, n, T * D, t * D, D),
                                                    ACT.Identity, bias=cut(shift, s, T, t, 1),
                                                    scale=cut(rstd, s, T, t, 1))
                    last.then_inc(u_act_ready, 1)
            turns(act, 8, turn)

            for n, (at, src) in enumerate(((0, 1), (3, 7))):
                act.wait_ge(routing_steps, (RT_MAX1, RT_MAX2)[n])
                nc.scalar.activation(route[:, (src + 2) * X:(src + 3) * X], route[:, src * X:(src + 1) * X],
                                     ACT.Exp, bias=small[:, at:at + 1],
                                     accum_out=small[:, at + 1:at + 2]).then_inc(routing_exps, 1)
            act.wait_ge(routing_steps, RT_DIFF)
            nc.scalar.activation(small[:, 8:9], small[:, 7:8], ACT.Exp).then_inc(routing_exps, 1)
            nc.scalar.preload_act_table(ACT.Gelu)

            def split_u(n, s):
                nc.scalar.copy(cut(uT_hi, s, G * N), cut(uT_sb, n, G * N)).then_inc(uT_hi_ready, 1)

            def choose_w1(s, g, offsets):
                for k in range(TOP):
                    chosen = w1_parts[:].rearrange("p (h e) -> p h e", h=2)[:, :, bass.ds(offsets[k], EW)]
                    last = nc.scalar.copy(cut(w1_sel, (s * G + g) * TOP + k, 2 * EW)
                                          .rearrange("p (h e) -> p h e", h=2), chosen)
                last.then_inc(w1_chosen, 1)

            for n in range(2):
                split_u(n, n)
            act.wait_ge(w1_lo_ready, 1)
            act.wait_ge(routing_steps, RT_OFFSETS)
            for m in range(G + 1):
                choose_w1(m // G, m % G, load_offsets(ACTIVATION, m, 1))
            act.wait_ge(routing_steps, RT_B1)

            def turn(n, s):
                more = 2 if not isinstance(n, int) else min(NP - 1 - n, 2)
                if more:
                    offsets = load_offsets(ACTIVATION, n * G + G + 1, more)
                for g in range(G):
                    act.wait_ge(hidden_ready, G * n + g + 1)
                    for k in range(TOP):
                        for c in range(FC):
                            last = nc.scalar.activation(
                                cut(hT, ((s * G + g) * TOP + k) * FC + c, N),
                                banks[2 * g + k][:, c * N:(c + 1) * N], ACT.Gelu,
                                bias=b1_sel[:, bass.ds(n * G + g + (c * TOP + k) * B, 1)])
                    last.then_inc(gelu_ready, 1)
                    if g == 0 and more:
                        choose_w1((s + 1) % 2, 1, offsets[0:TOP])
                if more == 2:
                    choose_w1(s, 0, offsets[TOP:2 * TOP])
                    split_u(n + 2, s)
            for n in range(2):
                turn(n, n)
            with act.Fori(1, NP // 2 - 1) as j:
                turn(2 * j, 0)
                turn(2 * j + 1, 1)
            for n in range(NP - 2, NP):
                turn(n, n % 2)

        @block.vector
        def _(dve):
            prep = [0]

            def chain(ins, s, n, hold=True):
                n[0] += 1
                ins.then_inc(s, 1)
                if hold:
                    dve.wait_ge(s, n[0])

            dve.wait_ge(edges_in, 32)
            dve.wait_ge(constants_set, CONSTANTS)
            chain(nc.vector.tensor_copy(edges_col_f[:], edges_col_i[:]), prep_steps, prep)
            chain(nc.vector.tensor_copy(edges_col_r[:], edges_col_f[:]), prep_steps, prep, False)
            chain(nc.vector.tensor_copy(ones_r[:], ones[:]), prep_steps, prep, False)
            chain(nc.vector.scalar_tensor_tensor(out=key_row[:], in0=edges_row_i[:], scalar=float(E),
                                                 in1=count_row[:], op0=ALU.mult, op1=ALU.add),
                  prep_steps, prep, False)
            chain(nc.vector.scalar_tensor_tensor(out=key_col[:], in0=edges_col_f[:, 0:K], scalar=float(E),
                                                 in1=edge_col[:], op0=ALU.mult, op1=ALU.add), prep_steps, prep)
            for k in range(K):
                chain(nc.vector.tensor_scalar(cut(before, k, E), key_row[:], key_col[:, k:k + 1], None,
                                              ALU.is_lt), prep_steps, prep, k == K - 1)
            chain(nc.vector.tensor_reduce(rank[:], before[:].rearrange("p (k e) -> p k e", k=K),
                                          AX.X, ALU.add), prep_steps, prep)
            for k in range(K):
                for q in range(2):
                    chain(nc.vector.tensor_scalar(cut(placed, 2 * k + q, E), count_row[:], rank[:, k:k + 1],
                                                  edges_col_f[:, q * K + k:q * K + k + 1],
                                                  ALU.is_equal, ALU.mult), prep_steps, prep, False)
            assert prep[0] == PREP_PLACED
            for k in range(K):
                chain(nc.vector.tensor_scalar(cut(place, k, E), count_row[:], rank[:, k:k + 1], None,
                                              ALU.is_equal), prep_steps, prep, False)
            assert prep[0] == PREP_PLACE

            def turn(i, r):
                if isinstance(i, int) and i in (0, 2):
                    dve.wait_ge(x_in[i // 2], 16)
                if live(i - 1):
                    dve.wait_ge(stats_ready, i)
                if live(i - 2):
                    n, s = i - 2, r
                    dve.wait_ge(scale_ready, n + 1)
                    normed(cut(z, s, T * D), cut(x_sb, n, T * D), s, range(C), z_dve_ready)
                if live(i - 1):
                    means((r + 1) % 2)
                if live(i):
                    statistics(cut(x_sb, i, T * D), r)
                if isinstance(i, int) and i == 2:
                    dve.wait_ge(sorted_copied, 1)
                    for c in range(C):
                        chain(nc.vector.tensor_scalar(cut(source_of, c, E), cut(sorted_row, 0, E),
                                                      node_col[:, c:c + 1], None, ALU.is_equal),
                              prep_steps, prep, False)
                    assert prep[0] == PREP_SOURCE
                if live(i - 2):
                    n, s = i - 2, r
                    dve.wait_ge(z_hi_ready, n + 1)
                    nc.vector.tensor_tensor(cut(z_lo, s, T * D), cut(z, s, T * D),
                                            cut(z_hi, s, T * D).bitcast(f32), ALU.subtract).then_inc(z_lo_ready, 1)
                if live(i - 5):
                    n, s = i - 5, (r + 1) % 2
                    dve.wait_ge(q_low_ready, n + 1)
                    nc.vector.tensor_tensor(cut(act_q, s, G * E), banks[4 + s], cut(q_low, s, G * E),
                                            ALU.max).then_inc(leaky_ready, 1)
                if isinstance(i, int) and i == NP + 4:
                    dve.wait_ge(leaky_ready, NP)
                    times_a(nc.vector, NP - 1, (NP - 1) % 2, last_weighed_ready)
                if live(i - 6):
                    n, s = i - 6, r
                    if isinstance(n, int) and n == NP - 1:
                        dve.wait_ge(last_weighed_ready, 1)
                    else:
                        dve.wait_ge(weighed_ready, n + 1)
                    nc.vector.tensor_reduce(cut(raw_logits, n, G * K * H),
                                            cut(weighed, s, G * K * D).rearrange("p (m d) -> p m d", d=DH),
                                            AX.X, ALU.add).then_inc(logits_ready, 1)
            for i in range(2):
                turn(i, i)
            dve.wait_ge(sorted_ready, 1)
            for c in range(C):
                chain(nc.vector.tensor_scalar(cut(gather, 2 * c + 1, E), banks[6][:, E:2 * E],
                                              node_col[:, c:c + 1], None, ALU.is_equal),
                      prep_steps, prep, c == C - 1)
            for c in range(C):
                chain(nc.vector.scalar_tensor_tensor(
                    out=cut(gather, 2 * c, E), in0=banks[6][:, 0:E], scalar=node_col[:, c:c + 1],
                    in1=cut(gather, 2 * c + 1, E).bitcast(f32), op0=ALU.is_equal, op1=ALU.add),
                    prep_steps, prep, False)
            assert prep[0] == PREP_GATHER
            for i in range(2, 4):
                turn(i, i % 2)
            dve.wait_ge(hots_ready, K)
            dve.wait_ge(adj_rows_ready, 1)
            nc.vector.tensor_tensor(adj_pick, banks[5], target_hot, ALU.mult).then_inc(adj_picked, 1)
            dve.wait_ge(adj_picked, 1)
            nc.vector.tensor_reduce(adj_edge[:], adj_pick.rearrange("p (k m) -> p k m", k=K),
                                    AX.X, ALU.add).then_inc(adj_picked, 1)
            nc.vector.tensor_tensor(same[:, 1:E], sorted_row[:, 1:E], sorted_row[:, 0:E - 1],
                                    ALU.is_equal).then_inc(same_ready, 1)
            for n in range(2, XCH):
                dve.wait_ge(x_in[n], 16)
            turns(dve, 6, turn, 4)

            sm = [0]
            dve.wait_ge(logits_ready, NP)
            dve.wait_ge(log_adj_ready, 1)
            for k in range(K):
                chain(nc.vector.tensor_scalar(
                    cut(logits_e, k, ROWS).rearrange("p (b h) -> p b h", h=H),
                    raw_logits[:].rearrange("p (b k h) -> p k b h", k=K, h=H)[:, k],
                    log_adj[:, k:k + 1], None, ALU.add), softmax_steps, sm, False)
            assert sm[0] == SM_LOGITS
            dve.wait_ge(softmax_turned, 1)
            dve.wait_ge(hots_ready, K + 2)
            logits = banks[5][0:ROWS, 0:E]
            chain(nc.vector.tensor_tensor_scan(scan[:], start_low[0:ROWS], logits, LOW, ALU.add, ALU.max),
                  softmax_steps, sm)
            chain(nc.vector.tensor_tensor(at_last[:], scan[:], is_last[0:ROWS], ALU.mult), softmax_steps, sm)
            chain(nc.vector.tensor_tensor_scan(seg_max[:, ::-1], same[0:ROWS, E:0:-1], at_last[:, ::-1], 0.0,
                                               ALU.mult, ALU.add), softmax_steps, sm)
            chain(nc.vector.tensor_tensor(shifted[:], logits, seg_max[:], ALU.subtract), softmax_steps, sm, False)
            assert sm[0] == SM_SHIFTED
            dve.wait_ge(exp_ready, 1)
            chain(nc.vector.tensor_tensor_scan(scan[:], same[0:ROWS, 0:E], expo[:], 0.0, ALU.mult, ALU.add),
                  softmax_steps, sm)
            chain(nc.vector.tensor_tensor(at_last[:], scan[:], is_last[0:ROWS], ALU.mult), softmax_steps, sm)
            chain(nc.vector.tensor_tensor_scan(seg_sum[:, ::-1], same[0:ROWS, E:0:-1], at_last[:, ::-1], 0.0,
                                               ALU.mult, ALU.add), softmax_steps, sm)
            chain(nc.vector.reciprocal(scan[:], seg_sum[:]), softmax_steps, sm)
            chain(nc.vector.tensor_tensor(attn[:], expo[:], scan[:], ALU.mult), softmax_steps, sm, False)
            assert sm[0] == SM_ATTN
            dve.wait_ge(softmax_turned, 2)
            chain(nc.vector.tensor_copy(attn_e[:].rearrange("p (b k h) -> p b k h", b=B, k=K),
                                        banks[5][:, 0:K * ROWS].rearrange("p (k b h) -> p b k h", k=K, b=B)),
                  softmax_steps, sm)

            dve.wait_ge(v_copied, NP)

            def scaled(n, s, i):
                dve.wait_ge(shift2_ready, n + 1)
                if isinstance(i, int) and i >= NP:
                    dve.wait_ge(u_turned, n - 1)
                for t in range(C):
                    last = nc.vector.tensor_scalar(cut(u, s * T + t, D), cut(x_sb, n, T * D, t * D, D),
                                                   cut(rstd, s, T, t, 1), cut(shift, s, T, t, 1),
                                                   ALU.mult, ALU.add)
                last.then_inc(u_dve_ready, 1)

            def turn(i, r):
                if live(i - 3):
                    n, s = i - 3, (r + 1) % 2
                    pair = cut(x_sb, n, T * D)
                    dve.wait_ge(gnn_ready, n + 1)
                    nc.vector.tensor_tensor(pair, banks[2 + s], pair, ALU.add).then_inc(x1_ready, 1)
                if live(i):
                    if isinstance(i, int) and i == 2:
                        dve.wait_ge(y_ready, 1)
                    weights = attn_e[:].rearrange("p (b k h) -> p (b k) h", b=B, k=K)
                    weights = weights[:, bass.ds(i * G * K, G * K)].unsqueeze(3)
                    nc.vector.tensor_tensor(
                        cut(av, r, G * K * D).rearrange("p (k h d) -> p k h d", k=G * K, h=H),
                        cut(v_sb, i, G * K * D).rearrange("p (k h d) -> p k h d", k=G * K, h=H),
                        weights.to_broadcast([P, G * K, H, DH]), ALU.mult).then_inc(av_ready, 1)
                if live(i - 3):
                    dve.wait_ge(x1_ready, i - 3 + 1)
                if live(i - 4):
                    dve.wait_ge(stats_ready, NP + i - 4 + 1)
                if live(i - 6):
                    scaled(i - 6, r, i)
                if live(i - 3):
                    statistics(cut(x_sb, i - 3, T * D), (r + 1) % 2)
                if live(i - 4) and not (isinstance(i, int) and i > NP + 1):
                    means(r)
                if isinstance(i, int) and i in (NP + 1, NP + 2):
                    dve.wait_ge(stats_ready, NP + i - 3 + 1)
                    dve.wait_ge(scale_ready, NP + i - 5 + 1)
                    means((r + 1) % 2)
            turns(dve, 6, turn)

            rt = [0]

            def col(n):
                return route[:, n * X:(n + 1) * X]

            def softmax(at, out_at, src, n_act):
                chain(nc.vector.tensor_reduce(small[:, at:at + 1], src, AX.X, ALU.max, negate=True),
                      routing_steps, rt, False)
                dve.wait_ge(routing_exps, n_act)
                chain(nc.vector.reciprocal(small[:, at + 2:at + 3], small[:, at + 1:at + 2]), routing_steps, rt)
                chain(nc.vector.tensor_scalar(col(out_at + 2), col(out_at + 1), small[:, at + 2:at + 3], None,
                                              ALU.mult), routing_steps, rt)

            dve.wait_ge(params_in, PARAMS)
            dve.wait_ge(routing_products, 1)
            chain(nc.vector.scalar_tensor_tensor(out=col(1), in0=banks[6][0:B, 0:X], scalar=1.0 / N,
                                                 in1=br_sb[:], op0=ALU.mult, op1=ALU.add), routing_steps, rt)
            softmax(0, 2, col(1), 1)
            assert rt[0] == RT_PROBS
            dve.wait_ge(routing_products, 2)
            chain(nc.vector.reciprocal(col(6), banks[7][0:B, 0:X]), routing_steps, rt)
            chain(nc.vector.tensor_scalar(col(6), col(6), CAPACITY / N, 1.0, ALU.mult, ALU.min), routing_steps, rt)
            chain(nc.vector.tensor_tensor(col(7), col(4), col(6), ALU.mult), routing_steps, rt)
            softmax(3, 8, col(7), 2)
            chain(nc.vector.max(col(11), col(10)), routing_steps, rt)
            chain(nc.vector.tensor_tensor(small[:, 7:8], route[:, 11 * X + 1:11 * X + 2],
                                          route[:, 11 * X:11 * X + 1], ALU.subtract), routing_steps, rt, False)
            assert rt[0] == RT_DIFF
            chain(nc.vector.max_index(top_i[:], col(11), col(10)), routing_steps, rt)
            chain(nc.vector.tensor_copy(col(12), top_i[:]), routing_steps, rt)
            chain(nc.vector.tensor_scalar(small[:, 12:12 + TOP], route[:, 12 * X:12 * X + TOP], float(EW),
                                          float((X - 1) * EW), ALU.mult, ALU.min), routing_steps, rt, False)
            dve.wait_ge(routing_exps, 3)
            chain(nc.vector.tensor_scalar(small[:, 9:10], small[:, 8:9], 1.0, None, ALU.add), routing_steps, rt)
            chain(nc.vector.reciprocal(small[:, 10:11], small[:, 9:10]), routing_steps, rt)
            chain(nc.vector.tensor_tensor(small[:, 11:12], small[:, 10:11], small[:, 8:9], ALU.mult), routing_steps, rt)
            chain(nc.vector.tensor_tensor(
                spread_w[:].rearrange("p (b q) -> p b q", q=2 * TOP),
                ident[0:B, 0:B].unsqueeze(2).to_broadcast([B, B, 2 * TOP]),
                small[:, 10:10 + 2 * TOP].unsqueeze(1).to_broadcast([B, B, 2 * TOP]), ALU.mult),
                routing_steps, rt, False)
            assert rt[0] == RT_SPREAD
            for k in range(TOP):
                chain(nc.vector.tensor_scalar(col(13 + k), count_row[0:B, 0:X],
                                              route[:, 12 * X + k:12 * X + k + 1], None,
                                              ALU.is_equal), routing_steps, rt, False)
            dve.wait_ge(routing_products, 3)
            chain(nc.vector.tensor_copy(
                offsets_i[:].rearrange("p (b k) -> p b k", k=TOP),
                banks[7][:, 0:B * 2 * TOP].rearrange("p (b q) -> p b q", q=2 * TOP)[:, :, TOP:2 * TOP]),
                routing_steps, rt, False)
            assert rt[0] == RT_OFFSETS
            chain(nc.vector.tensor_copy(weight_bc[:], banks[7][:, 0:B * 2 * TOP]), routing_steps, rt)
            chain(nc.vector.tensor_scalar(col(16), col(13), small[:, 10:11], None, ALU.mult), routing_steps, rt)
            chain(nc.vector.scalar_tensor_tensor(out=col(15), in0=col(14), scalar=small[:, 11:12], in1=col(16),
                                                 op0=ALU.mult, op1=ALU.add), routing_steps, rt, False)
            assert rt[0] == RT_DENSE
            dve.wait_ge(routing_products, 4)
            chain(nc.vector.tensor_copy(expertT[:], banks[6][0:X, 0:(TOP + 1) * B]), routing_steps, rt)
            assert rt[0] == RT_TURNED
            dve.wait_ge(routing_products, 5)
            chain(nc.vector.tensor_copy(b1_sel[:], banks[7][:, 0:FC * TOP * B]), routing_steps, rt, False)
            assert rt[0] == RT_B1
            chain(nc.vector.tensor_copy(b2_mix[:], banks[7][:, FC * TOP * B:(FC * TOP + 1) * B]), routing_steps, rt)

            dve.wait_ge(w2_in, 16)

            def scaled_rows(n, s):
                dve.wait_ge(scale_ready, 2 * NP + n + 1)
                dve.wait_ge(x_beta_ready, n + 1)
                if isinstance(n, int) and n >= NP - 2:
                    dve.wait_ge(centred_ready, n + 1)
                for t in range(T):
                    tile = cut(x_sb, n, T * D, t * D, D)
                    last = nc.vector.scalar_tensor_tensor(
                        out=tile, in0=cut(centred, s * T + t, D), scalar=cut(rstd, s, T, t, 1), in1=tile,
                        op0=ALU.mult, op1=ALU.add)
                last.then_inc(result_ready, 1)

            def turn(i, r):
                if live(i - 2):
                    n, s = i - 2, r
                    dve.wait_ge(ffn_ready, n + 1)
                    for g in range(G):
                        last = nc.vector.scalar_tensor_tensor(
                            out=cut(sT, s * G + g, N), in0=banks[4 + s][:, g * N:(g + 1) * N],
                            scalar=cut(b2_mix, n, G, g, 1), in1=cut(uT_sb, n, G * N, g * N, N),
                            op0=ALU.add, op1=ALU.add)
                    last.then_inc(sum_ready, 1)
                if live(i):
                    offsets = load_offsets(VECTOR, i * G)
                    for m in range(G * TOP):
                        g, k = m // TOP, m % TOP
                        if live(i - 2) and m == G * TOP - 1:
                            dve.wait_ge(sum_turned, i - 2 + 1)
                        last = nc.vector.tensor_scalar(
                            cut(w2_sel, r * G * TOP + m, FC * D), w2_sb[:, bass.ds(offsets[m], EW)],
                            cut(weight_bc, i, G * 2 * TOP, g * 2 * TOP + k, 1), None, ALU.mult)
                    last.then_inc(w2_chosen, 1)
                early = isinstance(i, int) and i == NP + 1
                if early:
                    scaled_rows(i - 3, (r + 1) % 2)
                if live(i - 2) and not live(i):
                    dve.wait_ge(sum_turned, i - 2 + 1)
                if live(i - 2):
                    statistics(banks[6 + r], r)
                    dve.wait_ge(stats_ready, 2 * NP + i - 2 + 1)
                if live(i - 3) and not early:
                    scaled_rows(i - 3, (r + 1) % 2)
                if live(i - 2):
                    means(r)
                    n, s = i - 2, r
                    dve.wait_ge(means_ready, 2 * NP + n + 1)
                    for t in range(T):
                        last = nc.vector.scalar_tensor_tensor(
                            out=cut(centred, s * T + t, D), in0=banks[6 + s][:, t * D:(t + 1) * D],
                            scalar=cut(mean_var, s, 2 * T, 2 * t, 1), in1=gamma_sb[:],
                            op0=ALU.subtract, op1=ALU.mult)
                    last.then_inc(centred_ready, 1)
            turns(dve, 3, turn)

        @block.tensor
        def _(pe):
            def mm(out_, lhsT, rhs, start=True, stop=True):
                return nc.tensor.matmul(out_, lhsT, rhs, start=start, stop=stop)

            def stay_warm(n, spare):
                for _ in range(n):
                    mm(spare[:, 0:N], ones[:], count_row[:])

            pe.wait_ge(constants_set, CONSTANTS)
            stay_warm(4, banks[0])
            pe.wait_ge(prep_steps, PREP_PLACED)
            for k in range(K):
                last = mm(banks[6], ones_r[:], cut(placed, k, 2 * E), k == 0, k == K - 1)
            last.then_inc(sorted_ready, 1)
            pe.wait_ge(prep_steps, PREP_PLACE)
            for j in range(K):
                for k in range(K):
                    last = mm(banks[7][:, 2 * j:2 * j + 2], cut(place, k, E, j * P, P),
                              edges_col_r[:].rearrange("p (q k) -> p k q", k=K)[:, k], k == 0, k == K - 1)
            last.then_inc(sorted_ready, 1)
            stay_warm(10, banks[0])
            pe.wait_ge(adj_in, 16)
            pe.wait_ge(prep_steps, PREP_SOURCE)
            for k in range(K):
                for c in range(C):
                    last = mm(banks[5][:, k * N:(k + 1) * N], cut(source_of, c, E, k * P, P),
                              cut(adj_sb, c, N), c == 0, c == C - 1)
            last.then_inc(adj_rows_ready, 1)
            pe.wait_ge(prep_steps, PREP_GATHER)
            pe.wait_ge(nets_in, 32)

            def turn(i, r):
                if live(i - 2):
                    n, s = i - 2, r
                    pe.wait_ge(z_lo_ready, n + 1)
                    for g in range(G):
                        for c in range(C):
                            for part in (z_hi, z_lo):
                                last = mm(banks[2 * s + g], cut(part, s * T + g * C + c, D),
                                          cut(gather, c, 2 * E),
                                          c == 0 and part is z_hi, c == C - 1 and part is z_lo)
                    last.then_inc(gather_ready, 1)
                if live(i - 3):
                    n, s = i - 3, (r + 1) % 2
                    pe.wait_ge(gathered_copied, n + 1)
                    if not isinstance(n, int) or n >= 2:
                        pe.wait_ge(leaky_ready, n - 1)
                        pe.wait_ge(v_copied, n - 1)
                    for g in range(G):
                        for k in range(K):
                            last = mm(banks[4 + s][:, (g * K + k) * D:(g * K + k + 1) * D],
                                      cut(gathered, s * G + g, 2 * E, k * P, P), W_LIN)
                    last.then_inc(q_ready, 1)
                    for g in range(G):
                        for k in range(K):
                            last = mm(banks[6 + s][:, (g * K + k) * D:(g * K + k + 1) * D],
                                      cut(gathered, s * G + g, 2 * E, E + k * P, P), W_VAL)
                    last.then_inc(v_ready, 1)
            for i in range(4):
                turn(i, i % 2)
            pe.wait_ge(adj_picked, 1)
            turns(pe, 3, turn, 4)

            pe.wait_ge(ident_set, 2)
            stay_warm(6, banks[3])
            pe.wait_ge(softmax_steps, SM_LOGITS)
            for k in range(K):
                last = nc.tensor.transpose(banks[5][0:ROWS, k * P:(k + 1) * P], cut(logits_e, k, ROWS), ident[:])
            last.then_inc(softmax_turned, 1)
            stay_warm(13, banks[3])
            pe.wait_ge(softmax_steps, SM_ATTN)
            for k in range(K):
                last = nc.tensor.transpose(banks[5][:, k * ROWS:(k + 1) * ROWS], attn[:, k * P:(k + 1) * P],
                                           ident[0:ROWS, 0:ROWS])
            last.then_inc(softmax_turned, 1)

            pe.wait_ge(hots_ready, 2 * K + 2)

            def turn(i, r):
                if isinstance(i, int) and i > NP + 1:
                    stay_warm(2, banks[0])
                if live(i - 7):
                    n, s = i - 7, (r + 1) % 2
                    pe.wait_ge(u_dve_ready, n + 1)
                    pe.wait_ge(u_act_ready, n + 1)
                    for t in range(T):
                        last = nc.tensor.transpose(banks[4 + s][:, t * P:(t + 1) * P],
                                                   cut(u, s * T + t, D), ident[:])
                    last.then_inc(u_turned, 1)
                if live(i - 1):
                    n, s = i - 1, (r + 1) % 2
                    pe.wait_ge(av_ready, n + 1)
                    for g in range(G):
                        for k in range(K):
                            last = mm(banks[s][:, g * N:(g + 1) * N], cut(av, (s * G + g) * K + k, D),
                                      cut(spread, k, N), k == 0, k == K - 1)
                    last.then_inc(y_ready, 1)
                if live(i - 2):
                    n, s = i - 2, r
                    pe.wait_ge(y_copied, n + 1)
                    if isinstance(n, int) and n == NP - 1:
                        pe.wait_ge(x1_ready, n - 1)
                    for t in range(T):
                        last = mm(banks[2 + s][:, t * D:(t + 1) * D], cut(yT, s * T + t, P), W_OUT)
                    last.then_inc(gnn_ready, 1)
            turns(pe, 7, turn)

            pe.wait_ge(params_in, PARAMS)
            pe.wait_ge(uT_ready, NP)
            mm(banks[6][0:B, 0:X], usum[:], router_sb[:]).then_inc(routing_products, 1)
            stay_warm(3, banks[0])
            pe.wait_ge(routing_steps, RT_PROBS)
            mm(banks[7][0:B, 0:X], ones[0:B, 0:B], route[:, 4 * X:5 * X]).then_inc(routing_products, 1)
            stay_warm(8, banks[0])
            pe.wait_ge(routing_steps, RT_SPREAD)
            mm(banks[7][:, 0:B * 2 * TOP], ones[0:B, :], spread_w[:]).then_inc(routing_products, 1)
            stay_warm(2, banks[0])
            pe.wait_ge(routing_steps, RT_DENSE)
            for m in range(TOP + 1):
                last = nc.tensor.transpose(banks[6][0:X, m * B:(m + 1) * B], route[:, (13 + m) * X:(14 + m) * X],
                                           ident[0:B, 0:B])
            last.then_inc(routing_products, 1)
            stay_warm(1, banks[0])
            pe.wait_ge(routing_steps, RT_TURNED)
            for c in range(FC):
                mm(banks[7][:, c * TOP * B:(c + 1) * TOP * B], biases_sb[:, c * P:(c + 1) * P], expertT[:, 0:TOP * B])
            mm(banks[7][:, FC * TOP * B:(FC * TOP + 1) * B], biases_sb[:, F:F + D],
               expertT[:, TOP * B:(TOP + 1) * B]).then_inc(routing_products, 1)

            def turned_back(n, s):
                pe.wait_ge(sum_ready, n + 1)
                for t in range(T):
                    last = nc.tensor.transpose(banks[6 + s][:, t * P:(t + 1) * P], cut(sT, s * T + t, P), ident[:])
                last.then_inc(sum_turned, 1)

            def turn(i, r):
                for g in range(G):
                    if live(i):
                        n, s = i, r
                        pe.wait_ge(w1_chosen, G * n + g + 1)
                        if g == 0:
                            pe.wait_ge(uT_lo_ready, n + 1)
                        if not isinstance(n, int) or n >= 1:
                            pe.wait_ge(gelu_ready, G * (n - 1) + g + 1)
                        for k in range(TOP):
                            for c in range(FC):
                                m = (s * G + g) * TOP + k
                                for half, part in ((0, uT_hi), (0, uT_lo), (1, uT_hi)):
                                    last = mm(banks[2 * g + k][:, c * N:(c + 1) * N],
                                              cut(w1_sel, 2 * m + half, EW, c * P, P),
                                              cut(part, s * G + g, N),
                                              (half, part) == (0, uT_hi), half == 1)
                        last.then_inc(hidden_ready, 1)
                    if live(i - 2) and g == 0:
                        turned_back(i - 2, r)
                    if live(i - 1):
                        n, s = i - 1, (r + 1) % 2
                        if g == 0:
                            pe.wait_ge(w2_chosen, n + 1)
                        pe.wait_ge(gelu_ready, G * n + g + 1)
                        for k in range(TOP):
                            for c in range(FC):
                                m = (s * G + g) * TOP + k
                                last = mm(banks[4 + s][:, g * N:(g + 1) * N], cut(w2_sel, m * FC + c, D),
                                          cut(hT, m * FC + c, N), k == 0 and c == 0,
                                          k == TOP - 1 and c == FC - 1)
                        if g == G - 1:
                            last.then_inc(ffn_ready, 1)
            turns(pe, 2, turn)


CONSTANTS = 10
PARAMS = 16 * 5

PREP_PLACED = 12
PREP_PLACE = 14
PREP_GATHER = 18
PREP_SOURCE = 20
SM_LOGITS = 2
SM_SHIFTED = 6
SM_ATTN = 11
RT_MAX1 = 2
RT_PROBS = 4
RT_MAX2 = 8
RT_DIFF = 12
RT_SPREAD = 19
RT_OFFSETS = 22
RT_DENSE = 25
RT_TURNED = 26
RT_B1 = 27


def kernel(**inputs):
    import numpy as np
    import concourse.bacc as bacc
    from concourse import mybir
    from concourse.bass_utils import run_bass_kernel_spmd

    get = {k: np.asarray(v) for k, v in inputs.items()}
    P = 128
    W1, b1, W2 = get["L0_ffn_W1"], get["L0_ffn_b1"], get["L0_ffn_W2"]
    X, D, F = W1.shape
    src, dst = get["L0_gnn_src"], get["L0_gnn_dst"]
    K = src.shape[0] // P
    arrays = {
        "x": get["x"],
        "adj": get["adj"],
        "nets": np.concatenate([get["L0_gnn_W_lin"].T, get["L0_gnn_W_val"].T, get["L0_gnn_W_out"].T], axis=1),
        "a_row": get["L0_gnn_a"].reshape(D),
        "router": get["L0_ffn_Wr"],
        "w1": W1.transpose(1, 0, 2).reshape(D, -1),
        "w2": W2.reshape(X, F // P, P, D).transpose(2, 0, 1, 3).reshape(P, -1),
        "edges_row": src.reshape(1, -1),
        "edges_col": np.concatenate([src.reshape(K, P).T, dst.reshape(K, P).T], axis=1),
        "br": get["L0_ffn_br"],
        "biases": np.concatenate([b1, get["L0_ffn_b2"]], axis=1),
        "gamma": get["L0_ffn_gamma"],
        "beta": get["L0_ffn_beta"],
    }
    nc = bacc.Bacc("TRN2", target_bir_lowering=False, num_devices=1)
    given, args = {}, []
    for name, a in arrays.items():
        a = np.ascontiguousarray(a)
        given[f"in_{name}"] = a
        args.append(nc.dram_tensor(f"in_{name}", a.shape, mybir.dt.from_np(a.dtype), kind="ExternalInput").ap())
    args.append(nc.dram_tensor("out_y", get["x"].shape, mybir.dt.float32, kind="ExternalOutput").ap())
    gnn_moe_program(nc, *args)
    r = run_bass_kernel_spmd(nc, [given], core_ids=[0])
    return r.results[0]["out_y"]
```
